# Optimizing a Trainium2 kernel written in Bass

```python
import numpy as np
import jax
import jax.numpy as jnp

def _softmax(x, axis=-1):
    return jax.nn.softmax(x, axis=axis)

def _gelu(x):
    return jax.nn.gelu(x, approximate=True)

def _silu(x):
    return jax.nn.silu(x)

def _sigmoid(x):
    return jax.nn.sigmoid(x)

def _layernorm(x, axis=-1, eps=1e-05):
    m = jnp.mean(x, axis=axis, keepdims=True)
    v = jnp.var(x, axis=axis, keepdims=True)
    return (x - m) / jnp.sqrt(v + eps)

def _scatter_add(tgt, idx, src, axis=0):
    return tgt.at[idx].add(src)

def _segment_sum(src, seg, n):
    return jax.ops.segment_sum(src, seg, n)
kernel_name = 'mk_gnn_preln_d2_gnn_r32_ccf119'

def setup_inputs(seed: int=0):
    np.random.seed(seed)
    _w = jnp.asarray

    def _rec_inputs():
        import jax
        import jax.numpy as jnp
        _gk = jax.random.key(seed)
        x = -0.0003713 + 1 * jax.random.normal(jax.random.fold_in(_gk, 1), (3125, 128), jnp.float32)
        _s = jax.random.randint(jax.random.fold_in(_gk, 2), (50000,), 0, 3125, jnp.int32)
        _d = jax.random.randint(jax.random.fold_in(_gk, 3), (50000,), 0, 3125, jnp.int32)
        _loop = jnp.arange(3125, dtype=jnp.int32)
        src = jnp.concatenate([_s, _d, _loop])
        dst = jnp.concatenate([_d, _s, _loop])
        _o = jnp.argsort(dst, stable=True)
        src = src[_o]
        dst = dst[_o]
        edge_type_32 = jax.random.randint(jax.random.fold_in(_gk, 13), (103125,), 0, 32, jnp.int32)
        edge_weight1 = jax.random.uniform(jax.random.fold_in(_gk, 14), (103125, 1), jnp.float32, 0.0, 0.999998)
        return (x, src, dst, edge_type_32, edge_weight1)
    x, src, dst, edge_type_32, edge_weight1 = _rec_inputs()

    def _L0_gnn_setup():
        import jax, jax.numpy as jnp
        import numpy as np
        N, E, DIN, H, C = (3125, 50000, 128, 8, 16)
        NEG_SLOPE = 0.2
        key = jax.random.key(seed)
        k1, k2, k3, k4, k5, k6 = jax.random.split(key, 6)
        x = jax.random.normal(k1, (N, DIN), dtype=jnp.float32)
        src = jax.random.randint(k2, (E,), 0, N, dtype=jnp.int64)
        dst = jax.random.randint(k3, (E,), 0, N, dtype=jnp.int64)
        dst = jnp.where(src == dst, (dst + 1) % N, dst)
        edge_index = jnp.stack([src, dst], axis=0)
        W = jax.random.normal(k4, (DIN, H * C), dtype=jnp.float32) * (1.0 / np.sqrt(DIN))
        att_src = jax.random.normal(k5, (H, C), dtype=jnp.float32) * (1.0 / np.sqrt(C))
        att_dst = jax.random.normal(k6, (H, C), dtype=jnp.float32) * (1.0 / np.sqrt(C))
        bias = jnp.zeros((H * C,), dtype=jnp.float32)
        return {'x': x, 'edge_index': edge_index, 'W': W, 'att_src': att_src, 'att_dst': att_dst, 'bias': bias}
    _L0_gnn_all = _L0_gnn_setup()
    _L0_gnn_in = {k: v for k, v in _L0_gnn_all.items() if k in ('W', 'att_src', 'att_dst', 'bias')}
    del _L0_gnn_all

    def _L1_gnn_setup():
        import jax, jax.numpy as jnp
        import numpy as np
        N, E, D, F, R, B = (50000, 50000, 128, 128, 32, 8)
        key = jax.random.key(seed)
        ks = jax.random.split(key, 9)
        h = jax.random.normal(ks[0], (N, D), dtype=jnp.float32)
        src = jax.random.randint(ks[1], (E,), 0, N, dtype=jnp.int32)
        dst = jax.random.randint(ks[2], (E,), 0, N, dtype=jnp.int32)
        etype = jax.random.randint(ks[3], (E,), 0, R, dtype=jnp.int32)
        norm = jax.random.uniform(ks[4], (E, 1), dtype=jnp.float32)
        weight = jax.random.normal(ks[5], (B, D, F), dtype=jnp.float32) * (2.0 / (D + F)) ** 0.5
        w_comp = jax.random.normal(ks[6], (R, B), dtype=jnp.float32) * (2.0 / (R + B)) ** 0.5
        loop_weight = jax.random.normal(ks[7], (D, F), dtype=jnp.float32) * (2.0 / (D + F)) ** 0.5
        h_bias = jnp.zeros((F,), dtype=jnp.float32)
        return {'h': h, 'src': src, 'dst': dst, 'etype': etype, 'norm': norm, 'weight': weight, 'w_comp': w_comp, 'loop_weight': loop_weight, 'h_bias': h_bias}
    _L1_gnn_all = _L1_gnn_setup()
    _L1_gnn_in = {k: v for k, v in _L1_gnn_all.items() if k in ('weight', 'w_comp', 'loop_weight', 'h_bias')}
    del _L1_gnn_all
    return {'x': x, 'src': src, 'dst': dst, 'edge_type_32': edge_type_32, 'edge_weight1': edge_weight1, 'L0_gnn_W': _L0_gnn_in['W'], 'L0_gnn_att_src': _L0_gnn_in['att_src'], 'L0_gnn_att_dst': _L0_gnn_in['att_dst'], 'L0_gnn_bias': _L0_gnn_in['bias'], 'L1_gnn_weight': _L1_gnn_in['weight'], 'L1_gnn_w_comp': _L1_gnn_in['w_comp'], 'L1_gnn_loop_weight': _L1_gnn_in['loop_weight'], 'L1_gnn_h_bias': _L1_gnn_in['h_bias']}

def reference(x, src, dst, edge_type_32, edge_weight1, L0_gnn_W, L0_gnn_att_src, L0_gnn_att_dst, L0_gnn_bias, L1_gnn_weight, L1_gnn_w_comp, L1_gnn_loop_weight, L1_gnn_h_bias):
    import jax
    import jax.numpy as jnp

    def _L0_gnn_ref(x, edge_index, W, att_src, att_dst, bias):
        import jax, jax.numpy as jnp
        import numpy as np
        N, E, DIN, H, C = (3125, 50000, 128, 8, 16)
        NEG_SLOPE = 0.2
        n = x.shape[0]
        h = (x @ W).reshape(n, H, C)
        a_src = jnp.einsum('nhc,hc->nh', h, att_src)
        a_dst = jnp.einsum('nhc,hc->nh', h, att_dst)
        loop = jnp.arange(n, dtype=edge_index.dtype)
        src = jnp.concatenate([edge_index[0], loop])
        dst = jnp.concatenate([edge_index[1], loop])
        e = jax.nn.leaky_relu(a_src[src] + a_dst[dst], NEG_SLOPE)
        m = jax.ops.segment_max(e, dst, num_segments=n)
        m = jnp.where(jnp.isfinite(m), m, 0.0)
        ex = jnp.exp(e - m[dst])
        denom = jax.ops.segment_sum(ex, dst, num_segments=n)
        alpha = ex / denom[dst]
        msg = h[src] * alpha[:, :, None]
        out = jax.ops.segment_sum(msg, dst, num_segments=n)
        return out.reshape(n, H * C) + bias

    def _L1_gnn_ref(h, src, dst, etype, norm, weight, w_comp, loop_weight, h_bias):
        import jax, jax.numpy as jnp
        import numpy as np
        N, E, D, F, R, B = (50000, 50000, 128, 128, 32, 8)
        n_nodes, d_in = h.shape
        n_rels = w_comp.shape[0]
        W_rel = jnp.einsum('rb,bdf->rdf', w_comp, weight)
        seg = etype * n_nodes + dst
        agg = jax.ops.segment_sum(h[src] * norm, seg, num_segments=n_rels * n_nodes)
        agg = agg.reshape(n_rels, n_nodes, d_in)
        node_repr = jnp.einsum('rnd,rdf->nf', agg, W_rel)
        node_repr = node_repr + h_bias + h @ loop_weight
        return jax.nn.relu(node_repr)
    edge_index = jnp.stack([src, dst])
    h = jnp.maximum(_layernorm(x, axis=-1), 0.0)
    x = x + _L0_gnn_ref(h, edge_index, L0_gnn_W, L0_gnn_att_src, L0_gnn_att_dst, L0_gnn_bias)
    h = jnp.maximum(_layernorm(x, axis=-1), 0.0)
    x = x + _L1_gnn_ref(h, src, dst, edge_type_32, edge_weight1, L1_gnn_weight, L1_gnn_w_comp, L1_gnn_loop_weight, L1_gnn_h_bias)
    return x

_drawn_inputs = setup_inputs


def setup_inputs(seed=0):
    import zlib

    import numpy as np

    out = dict(_drawn_inputs(seed))
    spreads = {'L0_gnn_bias': (0.0, 0.1), 'L1_gnn_h_bias': (0.0, 0.1)}
    factors = {}
    for name, (base, spread) in spreads.items():
        noise = np.random.default_rng([zlib.crc32(name.encode()), seed]).standard_normal(out[name].shape)
        drawn = base * np.exp(spread * noise) if base else spread * noise
        out[name] = jnp.asarray(drawn.astype(out[name].dtype))
    for name, factor in factors.items():
        out[name] = (out[name] * factor).astype(out[name].dtype)
    return out
```

```python
from contextlib import ExitStack

import concourse.bass as bass
from concourse import mybir

P = 128
N, E, D, H, C, R, B = 3125, 103125, 128, 8, 16, 32, 8
TILE = 128
G = 8
T = -(-E // (TILE * 2 * G)) * 2 * G
NI = T // (2 * G)
W0, S0 = 32, 4
W1, S1 = 16, 2
NB = -(-N // P)
NP = NB * P
CB = 5
NC = NB // CB
CW = CB * P
ROW0 = D + H
HW = D + 2 * H
SPREAD = 60.0
EPS = 1e-5
SLOPE = 0.2
VS = 15
M2 = 32 + H


def build(nc, x, src_t, dst_t, typ_t, wgt_t, w_att, att_src, att_dst, bias0, basis,
          w_comp, w_loop, bias1, out):
    f32, i32 = mybir.dt.float32, mybir.dt.int32
    ALU, ACT, AX = mybir.AluOpType, mybir.ActivationFunctionType, mybir.AxisListType
    ctx = ExitStack()
    with ctx:
        def sb(name, shape, dt=f32):
            return ctx.enter_context(nc.sbuf_tensor(name, shape, dt))

        def sem(name):
            return ctx.enter_context(nc.semaphore(name))

        table0 = nc.dram_tensor("table0", (NP, ROW0), f32, kind="Internal").ap()
        table1 = nc.dram_tensor("table1", (NP, D), f32, kind="Internal").ap()
        coef_row = nc.dram_tensor("coef_row", (TILE, B), f32, kind="Internal").ap()

        src_i = sb("src_i", [P, T + 2 * G], i32)
        dst_f = sb("dst_f", [P, T])
        loc0 = sb("loc0", [P, T])
        loc1 = sb("loc1", [P, T])
        typ_f = sb("typ_f", [P, T])
        wgt = sb("wgt", [P, T])
        xs = sb("xs", [P, NB * D])
        h1T = sb("h1T", [P, NP])
        hwT = sb("hwT", [P, NP])
        big = sb("big", [P, B * NP])
        agg1 = big[:, :].rearrange("p (b n) -> p b n", b=B)
        aggT = big[:, 0:NP]
        denT = big[:, NP:2 * NP]
        winT = big[:, 2 * NP:3 * NP]
        dscT = big[:, 3 * NP:4 * NP]
        sscT = big[:, 4 * NP:5 * NP]
        maxT = big[:, 5 * NP:6 * NP]
        hw = big[:, 6 * NP:6 * NP + NB * HW].rearrange("p (b f) -> p b f", b=NB)

        ones = sb("ones", [P, P])
        ident = sb("ident", [P, P])
        iota_i = sb("iota_i", [P, W0], i32)
        iota = sb("iota", [P, W0])
        quad = sb("quad", [P, 4])
        head_of = sb("head_of", [P, H])
        head_to = sb("head_to", [H, P])
        pick = sb("pick", [M2, 2 * H])
        w_sb = sb("w_sb", [P, D])
        wT = sb("wT", [P, D])
        att_c = sb("att_c", [P, 2])
        att_m = sb("att_m", [P, 2 * H])
        wcat = sb("wcat", [P, HW])
        w_dd = sb("w_dd", [P, M2])
        w_ss = sb("w_ss", [P, M2])
        comp4 = sb("comp4", [P, B])
        comp_bd = sb("comp_bd", [P, 4, B])
        basis_sb = sb("basis_sb", [P, B, D])
        loop_sb = sb("loop_sb", [P, D])
        bias0_b = sb("bias0_b", [P, D])
        bias1_b = sb("bias1_b", [P, D])
        eps_t = sb("eps_t", [P, 1])
        smax = sb("smax", [M2, 1])
        smin = sb("smin", [M2, 1])
        bad = sb("bad", [P, 4])
        mark = sb("mark", [P, 5])
        flag_f = sb("flag_f", [1, 1])
        flag = sb("flag", [1, 1], i32)
        msum = sb("msum", [P, CB])
        vsum = sb("vsum", [P, CB])
        rinv = sb("rinv", [P, CB])
        rstd = sb("rstd", [P, CB])

        work = sb("work", [P, 2 * G * ROW0 + G * D + 2 * G * D])
        g0 = work[:, 0:2 * G * ROW0].rearrange("p (s t f) -> p s t f", s=2, t=G)
        msg = work[:, 2 * G * ROW0:2 * G * ROW0 + G * D].rearrange("p (t f) -> p t f", t=G)
        g1 = work[:, 0:2 * G * D].rearrange("p (s t f) -> p s t f", s=2, t=G)
        sel1 = work[:, 2 * G * ROW0:2 * G * ROW0 + G * D].rearrange("p (t b w) -> p t b w", t=G, b=B)
        LNW = CW
        xm = work[:, 0:LNW]
        hc = work[:, LNW:2 * LNW]
        hcT = work[:, 2 * LNW:3 * LNW]
        sq = work[:, 3 * LNW:4 * LNW]
        tmp = work[:, 4 * LNW:5 * LNW]
        stg = work[:, 5 * LNW:6 * LNW]
        xm3, hc3, hcT3, sq3, tmp3 = (v.rearrange("p (b f) -> p b f", b=CB) for v in (xm, hc, hcT, sq, tmp))
        basei = big[:, 5 * NP:5 * NP + T].bitcast(i32)
        dst_i = big[:, 5 * NP + T:5 * NP + 2 * T].bitcast(i32)
        typ_i = big[:, 5 * NP + 2 * T:5 * NP + 3 * T].bitcast(i32)
        chk = big[:, 6 * NP + NB * HW:6 * NP + NB * HW + T]
        gz, gm, gp = xm[0:H, 0:TILE], sq[0:H, 0:TILE], tmp[0:H, 0:TILE]
        gcb = msg.rearrange("p t f -> p (t f)")
        aggc = work[:, 0:2 * B * P].rearrange("p (s b n) -> p s b n", s=2, b=B)
        h1c = work[:, 2 * B * P:2 * B * P + 2 * P].rearrange("p (s n) -> p s n", s=2)
        outc = work[:, 2 * B * P + 2 * P:2 * B * P + 4 * P].rearrange("p (s n) -> p s n", s=2)

        first = sb("first", [1, T], i32)
        idx = sb("idx", [P, 2, G], i32)
        oh = sb("oh", [P, G, W0])
        ohT = sb("ohT", [P, 2, P])
        awin = sb("awin", [M2, 2, 4, W0])
        bdw = sb("bdw", [P, 2, 4, 2 * H])
        zt = sb("zt", [P, G, H])
        lt = sb("lt", [P, G, H])
        pt = sb("pt", [P, G, H])
        oh1 = sb("oh1", [P, G, W1])
        coef = sb("coef", [P, G, B])
        dstg = sb("dstg", [H, CW])
        mstg = sb("mstg", [M2, CW])
        pself = sb("pself", [P, CB, H])
        zself = sb("zself", [P, CB, H])
        rself = sb("rself", [P, CB, H])

        ps = ctx.enter_context(nc.psum_tensor("ps", [P, 8 * 512], f32))

        def bank(k, cols, off=0):
            return ps[:, k * 512 + off:k * 512 + off + cols]

        s_const = sem("s_const")
        s_edges = sem("s_edges")
        s_x = sem("s_x")
        s_src = sem("s_src")
        s_gset = sem("s_gset")
        s_vset = sem("s_vset")
        s_pset = sem("s_pset")
        s_flag = sem("s_flag")
        s_hc = sem("s_hc")
        s_sqrt = sem("s_sqrt")
        s_var = sem("s_var")
        s_hcp = sem("s_hcp")
        s_hcT = sem("s_hcT")
        s_prj = sem("s_prj")
        s_prjc = sem("s_prjc")
        s_sc = sem("s_sc")
        s_scc = sem("s_scc")
        s_prT = sem("s_prT")
        s_prTc = sem("s_prTc")
        s_tab0 = sem("s_tab0")
        s_prep = sem("s_prep")
        got0 = [sem("got0_a"), sem("got0_b")]
        got1 = [sem("got1_a"), sem("got1_b")]
        s_idx = sem("s_idx")
        s_oh = sem("s_oh")
        s_ohp = sem("s_ohp")
        s_ohT = sem("s_ohT")
        s_awin = sem("s_awin")
        s_winp = sem("s_winp")
        s_bdw = sem("s_bdw")
        s_ade = sem("s_ade")
        s_log = sem("s_log")
        s_p = sem("s_p")
        s_msg = sem("s_msg")
        s_agg = sem("s_agg")
        s_v0 = sem("s_v0")
        s_l0 = sem("s_l0")
        s_idx1 = sem("s_idx1")
        s_oe = sem("s_oe")
        s_oep = sem("s_oep")
        s_oeT = sem("s_oeT")
        s_cop = sem("s_cop")
        s_sel = sem("s_sel")
        s_agg1 = sem("s_agg1")
        s_v1 = sem("s_v1")
        s_l1 = sem("s_l1")
        s_mst = sem("s_mst")
        s_mtp = sem("s_mtp")
        s_mlog = sem("s_mlog")
        s_mp = sem("s_mp")
        s_vm = sem("s_vm")
        s_vs = sem("s_vs")
        s_h1p = sem("s_h1p")
        s_h1T = sem("s_h1T")
        s_tab1 = sem("s_tab1")
        s_zero = sem("s_zero")
        s_fst = sem("s_fst")
        s_fp = sem("s_fp")
        s_fo = sem("s_fo")
        s_out = [sem("s_out_a"), sem("s_out_b")]
        s_gv = sem("s_gv")
        s_gz = sem("s_gz")
        s_gp = sem("s_gp")
        s_gb = sem("s_gb")
        s_gc = sem("s_gc")
        s_gw = sem("s_gw")
        s_gr = sem("s_gr")
        s_gu = sem("s_gu")

        block = ctx.enter_context(nc.Block())
        CONST_DMAS = 11
        EDGE_DMAS = 5

        @block.sync
        def _(sp):
            sp.dma_start(xs[:, :].rearrange("p (b f) -> p b f", b=NB),
                         x.rearrange("(b p) f -> p b f", p=P)).then_inc(s_x, 16)
            sp.dma_start(w_sb[:], w_att).then_inc(s_const, 16)
            sp.dma_start(att_c[:, 0:1], att_src.rearrange("h (c o) -> (h c) o", o=1)).then_inc(s_const, 16)
            sp.dma_start(att_c[:, 1:2], att_dst.rearrange("h (c o) -> (h c) o", o=1)).then_inc(s_const, 16)
            sp.dma_start(src_i[:], src_t).then_inc(s_src, 16)
            sp.dma_start(dst_i, dst_t).then_inc(s_edges, 16)
            sp.dma_start(basei, dst_t[0, :].partition_broadcast(P)).then_inc(s_edges, 16)
            sp.dma_start(first[:], dst_t[0:1, :]).then_inc(s_edges, 16)
            sp.dma_start(typ_i, typ_t).then_inc(s_edges, 16)
            sp.dma_start(wgt[:], wgt_t).then_inc(s_edges, 16)
            for q in range(4):
                sp.dma_start(comp4[32 * q:32 * q + R, :], w_comp).then_inc(s_const, 16)
            sp.dma_start(basis_sb[:], basis.rearrange("b d f -> d b f")).then_inc(s_const, 16)
            sp.dma_start(loop_sb[:], w_loop).then_inc(s_const, 16)
            sp.dma_start(bias0_b[:], bias0.partition_broadcast(P)).then_inc(s_const, 16)
            sp.dma_start(bias1_b[:], bias1.partition_broadcast(P)).then_inc(s_const, 16)
            with sp.Fori(0, NC) as c:
                sp.wait_ge(s_prjc, c + 1)
                sp.dma_start(table0[bass.ds(c * CW, CW), :].rearrange("(b p) f -> p b f", p=P),
                             hw[:, bass.ds(c * CB, CB), 0:ROW0]).then_inc(s_tab0, 16)
            with sp.Fori(0, NC) as c:
                sp.wait_ge(s_hc, c + NC + 1)
                sp.dma_start(table1[bass.ds(c * CW, CW), :].rearrange("(b p) f -> p b f", p=P),
                             hc.rearrange("p (b f) -> p b f", b=CB)).then_inc(s_tab1, 16)
            sp.wait_ge(s_flag, 1)
            general = sp.value_load(flag[0:1, 0:1], min_val=0, max_val=1)
            with sp.If(general > 0):
                with sp.Fori(0, T) as t:
                    sp.wait_ge(s_gc, t + 1)
                    sp.dma_start(coef_row, coef[:, 0, :]).then_inc(s_gw, 16)
                    sp.wait_ge(s_gw, t * 16 + 16)
                    sp.dma_start(msg.rearrange("p t f -> p (t f)"),
                                 coef_row.rearrange("(o e) b -> o (e b)", o=1)[0].partition_broadcast(P)
                                 ).then_inc(s_gr, 16)

            def store(n, s):
                sp.wait_ge(s_fo, n + 3)
                sp.dma_start(out[bass.ds(n * P, P), :] if not isinstance(n, int) else out[n * P:n * P + P, :],
                             outc[:, s, :]).then_inc(s_out[s], 16)

            with sp.Fori(0, NB // 2) as i:
                store(i * 2, 0)
                store(i * 2 + 1, 1)
            store(NB - 1, 0)
            sp.wait_ge(s_out[0], 16 * (NB // 2 + 1))
            sp.wait_ge(s_out[1], 16 * (NB // 2))

        @block.gpsimd
        def _(pool):
            nc.gpsimd.iota(iota_i[:], pattern=[[1, W0]], base=0, channel_multiplier=0).then_inc(s_gset, 1)
            nc.gpsimd.memset(ones[:], 1.0).then_inc(s_gset, 1)
            pool.wait_ge(s_gset, 2)
            nc.gpsimd.affine_select(out=ident[:], in_=ones[:], pattern=[[-1, P]], base=0, channel_multiplier=1,
                                    compare_op=ALU.is_equal, fill=0.0).then_inc(s_gset, 1)
            nc.gpsimd.affine_select(out=quad[:], in_=ones[:, 0:4], pattern=[[-32, 4]], base=0,
                                    channel_multiplier=1, compare_op=ALU.is_ge, fill=0.0).then_inc(s_gset, 1)
            nc.gpsimd.affine_select(out=head_of[:], in_=ones[:, 0:H], pattern=[[-C, H]], base=0,
                                    channel_multiplier=1, compare_op=ALU.is_ge, fill=0.0).then_inc(s_gset, 1)
            nc.gpsimd.affine_select(out=head_to[:], in_=ones[0:H, :], pattern=[[1, P]], base=0,
                                    channel_multiplier=-C, compare_op=ALU.is_ge, fill=0.0).then_inc(s_gset, 1)
            nc.gpsimd.affine_select(out=pick[:, 0:H], in_=ones[0:M2, 0:H], pattern=[[-1, H]], base=0,
                                    channel_multiplier=1, compare_op=ALU.is_equal, fill=0.0).then_inc(s_gset, 1)
            nc.gpsimd.affine_select(out=pick[:, H:2 * H], in_=ones[0:M2, 0:H], pattern=[[-1, H]], base=-32,
                                    channel_multiplier=1, compare_op=ALU.is_equal, fill=0.0).then_inc(s_gset, 1)
            pool.wait_ge(s_gset, 8)
            nc.gpsimd.affine_select(out=quad[:], in_=quad[:], pattern=[[32, 4]], base=31,
                                    channel_multiplier=-1, compare_op=ALU.is_ge, fill=0.0).then_inc(s_gset, 1)
            nc.gpsimd.affine_select(out=head_of[:], in_=head_of[:], pattern=[[C, H]], base=C - 1,
                                    channel_multiplier=-1, compare_op=ALU.is_ge, fill=0.0).then_inc(s_gset, 1)
            nc.gpsimd.affine_select(out=head_to[:], in_=head_to[:], pattern=[[-1, P]], base=C - 1,
                                    channel_multiplier=C, compare_op=ALU.is_ge, fill=0.0).then_inc(s_gset, 1)
            nc.gpsimd.memset(aggT, 0.0).then_inc(s_gset, 1)
            nc.gpsimd.memset(denT[0:H], 0.0).then_inc(s_gset, 1)
            nc.gpsimd.memset(winT[0:M2], 0.0).then_inc(s_gset, 1)

            pool.wait_ge(s_flag, 1)
            general = pool.value_load(flag[0:1, 0:1], min_val=0, max_val=1)

            def gather_loop(table, g, got, staged):
                with pool.Fori(0, NI) as i:
                    for s in range(2):
                        pool.wait_ge(staged, i * 2 + s + 1)
                        pool.nop(nofuse=True)
                        for t in range(G):
                            nc.gpsimd.indirect_dma_start(
                                out=g[:, s, t, :], out_offset=None, in_=table,
                                in_offset=bass.IndirectOffsetOnAxis(ap=idx[:, s, t:t + 1], axis=0),
                            ).then_inc(got[s], 16)

            pool.wait_ge(s_tab0, 16 * NC)
            with pool.If(general < 1):
                gather_loop(table0, g0, got0, s_idx)
            pool.wait_ge(s_tab1, 16 * NC)
            with pool.If(general < 1):
                gather_loop(table1, g1, got1, s_idx1)

        @block.scalar
        def _(act):
            with act.Fori(0, NC) as c:
                act.wait_ge(s_var, c + 1)
                nc.scalar.activation(rstd[:], vsum[:], ACT.Sqrt, bias=eps_t[:], scale=1.0 / D).then_inc(s_sqrt, 1)
                act.wait_ge(s_hcp, c + 1)
                nc.scalar.copy(hcT, bank(0, CW)).then_inc(s_hcT, 1)
                act.wait_ge(s_prj, c + 1)
                nc.scalar.copy(hw[:, bass.ds(c * CB, CB), :],
                               ps[:, 1024:1024 + CB * 256].rearrange("p (b f) -> p b f", b=CB)[:, :, 0:HW]
                               ).then_inc(s_prjc, 1)
                act.wait_ge(s_prT, c + 1)
                nc.scalar.copy(hwT[:, bass.ds(c * CW, CW)], bank(5, CW)).then_inc(s_prTc, 1)
            act.wait_ge(s_src, 16)
            act.wait_ge(s_flag, 1)
            general = act.value_load(flag[0:1, 0:1], min_val=0, max_val=1)

            def stage(gi, s, staged):
                nc.scalar.copy(idx[:, s, :], src_i[:, bass.ds(gi * G, G)]).then_inc(staged, 1)

            with act.If(general < 1):
                stage(0, 0, s_idx)
                stage(1, 1, s_idx)
                act.wait_ge(s_prep, 1)
                with act.Fori(0, NI) as i:
                    for s in range(2):
                        gi = i * 2 + s
                        for k in range(2):
                            n0 = act.value_load(first[0:1, bass.ds(gi * G + k * S0, 1)], min_val=0, max_val=N)
                            last = nc.scalar.copy(awin[:, k, :, :],
                                                  winT[0:M2, bass.ds(n0, W0)].unsqueeze(1).to_broadcast([M2, 4, W0]))
                        last.then_inc(s_awin, 1)
                        act.wait_ge(s_ohp, gi + 1)
                        nc.scalar.copy(ohT[:].rearrange("p s e -> p (s e)"), bank(0, 2 * P)).then_inc(s_ohT, 1)
                        act.wait_ge(s_log, gi + 1)
                        nc.scalar.activation(pt[:], zt[:], ACT.Exp).then_inc(s_p, 1)
                        act.wait_ge(s_msg, gi + 1)
                        stage(gi + 2, s, s_idx)
            with act.If(general > 0):
                with act.Fori(0, T) as t:
                    act.wait_ge(s_gz, t + 1)
                    nc.scalar.activation(gp, gz, ACT.Exp).then_inc(s_gp, 1)
            act.wait_ge(s_l0, 1)
            with act.Fori(0, NC) as c:
                act.wait_ge(s_vm, c * 9 + 1)
                nc.scalar.copy(stg, aggT[:, bass.ds(c * CW, CW)]).then_inc(s_mst, 1)
                nc.scalar.copy(dstg[:], denT[0:H, bass.ds(c * CW, CW)]).then_inc(s_mst, 1)
                nc.scalar.copy(mstg[32:M2, :], winT[32:M2, bass.ds(c * CW, CW)]).then_inc(s_mst, 1)
                act.wait_ge(s_mlog, c + 1)
                nc.scalar.activation(pself[:], zself[:], ACT.Exp).then_inc(s_mp, 1)
                act.wait_ge(s_var, c + NC + 1)
                nc.scalar.activation(rstd[:], vsum[:], ACT.Sqrt, bias=eps_t[:], scale=1.0 / D).then_inc(s_sqrt, 1)
                act.wait_ge(s_h1p, c + 1)
                nc.scalar.copy(h1T[:, bass.ds(c * CW, CW)], bank(0, CW)).then_inc(s_h1T, 1)
            with act.If(general < 1):
                stage(0, 0, s_idx1)
                stage(1, 1, s_idx1)
                with act.Fori(0, NI) as i:
                    for s in range(2):
                        gi = i * 2 + s
                        act.wait_ge(s_oep, gi + 1)
                        nc.scalar.copy(ohT[:].rearrange("p s e -> p (s e)"), bank(0, 2 * P)).then_inc(s_oeT, 1)
                        act.wait_ge(s_agg1, gi + 1)
                        stage(gi + 2, s, s_idx1)
            act.wait_ge(s_l1, 1)

            def stage_block(n, s):
                act.wait_ge(s_fp, n + 1)
                nc.scalar.copy(aggc[:, s], agg1[:, :, bass.ds(n * P, P)] if not isinstance(n, int)
                               else agg1[:, :, n * P:n * P + P]).then_inc(s_fst, 1)
                nc.scalar.copy(h1c[:, s], h1T[:, bass.ds(n * P, P)] if not isinstance(n, int)
                               else h1T[:, n * P:n * P + P]).then_inc(s_fst, 1)

            with act.Fori(0, NB // 2) as i:
                stage_block(i * 2, 0)
                stage_block(i * 2 + 1, 1)
            stage_block(NB - 1, 0)

        @block.vector
        def _(dve):
            def layernorm(c, chunk):
                xv = xs[:, bass.ds(c * CW, CW)].rearrange("p (b f) -> p b f", b=CB)
                base = chunk * 4
                nc.vector.tensor_reduce(out=msum[:], in_=xv, axis=AX.X, op=ALU.add).then_inc(s_vs, 1)
                dve.wait_ge(s_vs, base + 1)
                nc.vector.scalar_tensor_tensor(out=xm3, in0=msum[:].unsqueeze(2).to_broadcast([P, CB, D]),
                                               scalar=-1.0 / D, in1=xv, op0=ALU.mult, op1=ALU.add).then_inc(s_vs, 1)
                dve.wait_ge(s_vs, base + 2)
                nc.vector.tensor_tensor(out=sq3, in0=xm3, in1=xm3, op=ALU.mult).then_inc(s_vs, 1)
                dve.wait_ge(s_vs, base + 3)
                nc.vector.tensor_reduce(out=vsum[:], in_=sq3, axis=AX.X, op=ALU.add).then_inc(s_var, 1)
                dve.wait_ge(s_sqrt, chunk + 1)
                nc.vector.reciprocal(rinv[:], rstd[:]).then_inc(s_vs, 1)
                dve.wait_ge(s_vs, base + 4)
                nc.vector.scalar_tensor_tensor(out=hc3, in0=xm3, scalar=0.0,
                                               in1=rinv[:].unsqueeze(2).to_broadcast([P, CB, D]),
                                               op0=ALU.max, op1=ALU.mult).then_inc(s_hc, 1)

            nc.vector.memset(eps_t[:], EPS).then_inc(s_vset, 1)
            nc.vector.memset(w_dd[:], 0.0).then_inc(s_vset, 1)
            nc.vector.memset(w_ss[:], 0.0).then_inc(s_vset, 1)
            nc.vector.memset(bad[:], 0.0).then_inc(s_vset, 1)
            dve.wait_ge(s_gset, 14)
            dve.wait_ge(s_const, 16 * CONST_DMAS)
            nc.vector.tensor_copy(iota[:], iota_i[:]).then_inc(s_vset, 1)
            for k in range(2):
                nc.vector.tensor_tensor(out=att_m[:, k * H:k * H + H], in0=head_of[:],
                                        in1=att_c[:, k:k + 1].to_broadcast([P, H]), op=ALU.mult).then_inc(s_vset, 1)
            nc.vector.tensor_tensor(out=comp_bd[:], in0=quad[:].unsqueeze(2).to_broadcast([P, 4, B]),
                                    in1=comp4[:].unsqueeze(1).to_broadcast([P, 4, B]), op=ALU.mult).then_inc(s_vset, 1)
            nc.vector.tensor_copy(wcat[:, 0:D], w_sb[:]).then_inc(s_vset, 1)
            dve.wait_ge(s_pset, 1)
            nc.vector.tensor_copy(wT[:], bank(0, P)).then_inc(s_vset, 1)
            dve.wait_ge(s_pset, 2)
            nc.vector.tensor_copy(wcat[:, D:HW], bank(1, 2 * H)).then_inc(s_vset, 1)
            for k in (0, 32):
                nc.vector.tensor_copy(w_ss[:, k:k + H], bank(1, H)).then_inc(s_vset, 1)
                nc.vector.tensor_copy(w_dd[:, k:k + H], bank(1, H, H)).then_inc(s_vset, 1)

            dve.wait_ge(s_edges, 16 * EDGE_DMAS)
            nc.vector.tensor_copy(dst_f[:], dst_i).then_inc(s_vset, 1)
            nc.vector.tensor_copy(typ_f[:], typ_i).then_inc(s_vset, 1)
            for loc, sh in ((loc0, S0), (loc1, S1)):
                nc.vector.tensor_tensor(
                    out=loc[:].rearrange("p (k j) -> p k j", j=sh), in0=dst_i.rearrange("p (k j) -> p k j", j=sh),
                    in1=basei.rearrange("p (k j) -> p k j", j=sh)[:, :, 0:1].to_broadcast([P, T // sh, sh]),
                    op=ALU.subtract).then_inc(s_vset, 1)
            dve.wait_ge(s_vset, VS + 4)
            nc.vector.tensor_scalar(out=chk, in0=loc0[:], scalar1=0.0, scalar2=None, op0=ALU.is_lt).then_inc(s_vset, 1)
            for n, (loc, lim, op) in enumerate(((loc0, W0 - 1.0, ALU.is_gt), (loc1, 0.0, ALU.is_lt),
                                                (loc1, W1 - 1.0, ALU.is_gt))):
                dve.wait_ge(s_vset, VS + 5 + n)
                nc.vector.scalar_tensor_tensor(out=chk, in0=loc[:], scalar=lim, in1=chk, op0=op,
                                               op1=ALU.add).then_inc(s_vset, 1)
            dve.wait_ge(s_vset, VS + 8)
            nc.vector.scalar_tensor_tensor(out=chk, in0=dst_f[:], scalar=float(N), in1=chk, op0=ALU.is_lt,
                                           op1=ALU.mult).then_inc(s_vset, 1)
            dve.wait_ge(s_vset, VS + 9)
            nc.vector.tensor_reduce(out=bad[:, 0:1], in_=chk, axis=AX.X, op=ALU.max).then_inc(s_vset, 1)

            dve.wait_ge(s_x, 16)
            with dve.Fori(0, NC) as c:
                layernorm(c, c)
                dve.wait_ge(s_sc, c + 1)
                nc.vector.tensor_copy(dscT[0:M2, bass.ds(c * CW, CW)], bank(5, CW)[0:M2])
                nc.vector.tensor_copy(sscT[0:M2, bass.ds(c * CW, CW)], bank(0, CW)[0:M2]).then_inc(s_scc, 1)

            dve.wait_ge(s_scc, NC)
            nc.vector.tensor_reduce(out=smax[:], in_=sscT[0:M2, 0:N], axis=AX.X, op=ALU.max).then_inc(s_vset, 1)
            nc.vector.tensor_reduce(out=smin[:], in_=sscT[0:M2, 0:N], axis=AX.X, op=ALU.min).then_inc(s_vset, 1)
            dve.wait_ge(s_vset, VS + 12)
            nc.vector.tensor_scalar(out=bad[0:H, 1:2], in0=smax[0:H], scalar1=smin[0:H], scalar2=SPREAD,
                                    op0=ALU.subtract, op1=ALU.is_gt).then_inc(s_vset, 1)
            dve.wait_ge(s_pset, 3)
            nc.vector.tensor_reduce(out=flag_f[:], in_=bank(7, 2)[0:1], axis=AX.X, op=ALU.add).then_inc(s_vset, 1)
            dve.wait_ge(s_vset, VS + 14)
            nc.vector.tensor_scalar(out=flag[:], in0=flag_f[:], scalar1=0.0, scalar2=None,
                                    op0=ALU.is_gt).then_inc(s_flag, 1)
            dve.wait_ge(s_flag, 1)
            general = dve.value_load(flag[0:1, 0:1], min_val=0, max_val=1)

            with dve.If(general < 1):
                nc.vector.tensor_scalar(out=maxT[0:M2, :], in0=dscT[0:M2, :], scalar1=smax[:], scalar2=None,
                                        op0=ALU.add).then_inc(s_vset, 1)
            with dve.If(general > 0):
                nc.vector.tensor_copy(maxT[0:M2, :], sscT[0:M2, :]).then_inc(s_gv, 1)
                dve.wait_ge(s_gv, 1)
                dve.sem_clear(s_gv)
                with dve.Fori(0, T) as t:
                    with dve.Fori(0, TILE) as e:
                        u = dve.value_load(src_t[bass.ds(e, 1), bass.ds(t, 1)], min_val=0, max_val=N - 1)
                        v = dve.value_load(dst_t[bass.ds(e, 1), bass.ds(t, 1)], min_val=0, max_val=N)
                        nc.vector.tensor_tensor(out=maxT[0:M2, bass.ds(v, 1)], in0=maxT[0:M2, bass.ds(v, 1)],
                                                in1=sscT[0:M2, bass.ds(u, 1)], op=ALU.max).then_inc(s_gv, 1)
                        dve.wait_ge(s_gv, e + 1)
                        dve.nop(nofuse=True)
                    dve.sem_clear(s_gv)
                nc.vector.tensor_tensor(out=maxT[0:M2, :], in0=maxT[0:M2, :], in1=dscT[0:M2, :],
                                        op=ALU.add).then_inc(s_vset, 1)
            dve.wait_ge(s_vset, VS + 15)
            nc.vector.tensor_copy(winT[0:H, :], dscT[0:H, :])
            nc.vector.scalar_tensor_tensor(out=winT[32:M2, :], in0=maxT[32:M2, :], scalar=SLOPE, in1=maxT[32:M2, :],
                                           op0=ALU.mult, op1=ALU.max).then_inc(s_prep, 1)

            with dve.If(general < 1):
                with dve.Fori(0, NI) as i:
                    for s in range(2):
                        gi = i * 2 + s
                        step = gi * 7
                        nc.vector.tensor_tensor(
                            out=oh[:], in0=loc0[:, bass.ds(gi * G, G)].unsqueeze(2).to_broadcast([P, G, W0]),
                            in1=iota[:].unsqueeze(1).to_broadcast([P, G, W0]), op=ALU.is_equal).then_inc(s_oh, 1)
                        n0 = [dve.value_load(first[0:1, bass.ds(gi * G + k * S0, 1)], min_val=0, max_val=N)
                              for k in range(2)]
                        dve.wait_ge(s_winp, gi + 1)
                        nc.vector.tensor_tensor(
                            out=bdw[:], in0=bank(1, 4 * H).rearrange("p (k h) -> p k h", k=2).unsqueeze(2)
                            .to_broadcast([P, 2, 4, 2 * H]),
                            in1=quad[:].unsqueeze(1).unsqueeze(3).to_broadcast([P, 2, 4, 2 * H]),
                            op=ALU.mult).then_inc(s_bdw, 1)
                        ade = bank(2, 2 * 4 * 2 * H).rearrange("p (t h) -> p t h", t=G)
                        dve.wait_ge(got0[s], i * (16 * G) + 16 * G)
                        dve.wait_ge(s_ade, gi + 1)
                        nc.vector.tensor_tensor(out=zt[:], in0=g0[:, s, :, D:ROW0], in1=ade[:, :, 0:H],
                                                op=ALU.add).then_inc(s_v0, 1)
                        dve.wait_ge(s_v0, step + 1)
                        nc.vector.scalar_tensor_tensor(out=lt[:], in0=zt[:], scalar=SLOPE, in1=zt[:], op0=ALU.mult,
                                                       op1=ALU.max).then_inc(s_v0, 1)
                        dve.wait_ge(s_v0, step + 2)
                        nc.vector.tensor_tensor(out=lt[:], in0=lt[:], in1=ade[:, :, H:2 * H],
                                                op=ALU.subtract).then_inc(s_v0, 1)
                        dve.wait_ge(s_v0, step + 3)
                        nc.vector.tensor_scalar(out=zt[:], in0=lt[:], scalar1=0.0, scalar2=None,
                                                op0=ALU.min).then_inc(s_log, 1)
                        dve.wait_ge(s_p, gi + 1)
                        nc.vector.tensor_tensor(
                            out=msg.rearrange("p t (h c) -> p t h c", h=H),
                            in0=g0[:, s, :, 0:D].rearrange("p t (h c) -> p t h c", h=H),
                            in1=pt[:].unsqueeze(3).to_broadcast([P, G, H, C]), op=ALU.mult).then_inc(s_msg, 1)
                        dve.wait_ge(s_agg, gi + 1)
                        for k in range(2):
                            if k:
                                dve.wait_ge(s_v0, step + 5)
                            for table, part in ((aggT[:, bass.ds(n0[k], W0)], bank(3, W0, k * W0)),
                                                (denT[0:H, bass.ds(n0[k], W0)], bank(4, W0, k * W0)[0:H])):
                                nc.vector.tensor_tensor(out=table, in0=table, in1=part, op=ALU.add).then_inc(s_v0, 1)
                dve.wait_ge(s_v0, 14 * NI)
            with dve.If(general > 0):
                nc.vector.scalar_tensor_tensor(out=maxT[0:M2, :], in0=maxT[0:M2, :], scalar=SLOPE,
                                               in1=maxT[0:M2, :], op0=ALU.mult, op1=ALU.max).then_inc(s_gv, 1)
                dve.wait_ge(s_gv, 1)
                dve.sem_clear(s_gv)
                with dve.Fori(0, T) as t:
                    with dve.Fori(0, TILE) as e:
                        u = dve.value_load(src_t[bass.ds(e, 1), bass.ds(t, 1)], min_val=0, max_val=N - 1)
                        v = dve.value_load(dst_t[bass.ds(e, 1), bass.ds(t, 1)], min_val=0, max_val=N)
                        nc.vector.tensor_tensor(out=gz[:, bass.ds(e, 1)], in0=sscT[0:H, bass.ds(u, 1)],
                                                in1=dscT[0:H, bass.ds(v, 1)], op=ALU.add)
                        nc.vector.tensor_copy(gm[:, bass.ds(e, 1)], maxT[0:H, bass.ds(v, 1)]).then_inc(s_gv, 1)
                    dve.wait_ge(s_gv, TILE)
                    nc.vector.scalar_tensor_tensor(out=gz, in0=gz, scalar=SLOPE, in1=gz, op0=ALU.mult,
                                                   op1=ALU.max).then_inc(s_gv, 1)
                    dve.wait_ge(s_gv, TILE + 1)
                    nc.vector.tensor_tensor(out=gz, in0=gz, in1=gm, op=ALU.subtract).then_inc(s_gz, 1)
                    dve.wait_ge(s_gb, t + 1)
                    dve.nop(nofuse=True)
                    dve.sem_clear(s_gv)
                    with dve.Fori(0, TILE) as e:
                        u = dve.value_load(src_t[bass.ds(e, 1), bass.ds(t, 1)], min_val=0, max_val=N - 1)
                        v = dve.value_load(dst_t[bass.ds(e, 1), bass.ds(t, 1)], min_val=0, max_val=N)
                        nc.vector.tensor_tensor(out=denT[0:H, bass.ds(v, 1)], in0=denT[0:H, bass.ds(v, 1)],
                                                in1=gp[:, bass.ds(e, 1)], op=ALU.add)
                        nc.vector.scalar_tensor_tensor(
                            out=aggT[:, bass.ds(v, 1)], in0=hwT[:, bass.ds(u, 1)], scalar=ps[:, bass.ds(e, 1)],
                            in1=aggT[:, bass.ds(v, 1)], op0=ALU.mult, op1=ALU.add).then_inc(s_gv, 1)
                        dve.wait_ge(s_gv, e + 1)
                        dve.nop(nofuse=True)
                    dve.sem_clear(s_gv)
            nc.vector.memset(mark[:, 0:1], 0.0).then_inc(s_l0, 1)
            nc.vector.memset(mark[:, 1:2], 0.0).then_inc(s_vm, 1)

            with dve.Fori(0, NC) as c:
                hwc = hw[:, bass.ds(c * CB, CB), :]
                xv = xs[:, bass.ds(c * CW, CW)].rearrange("p (b f) -> p b f", b=CB)
                shf = bank(2, CB * H).rearrange("p (b h) -> p b h", b=CB)
                den = bank(3, CB * H).rearrange("p (b h) -> p b h", b=CB)
                num = bank(4, CW).rearrange("p (b f) -> p b f", b=CB)
                base = c * 9 + 1
                nc.vector.tensor_tensor(out=zself[:], in0=hwc[:, :, D:ROW0], in1=hwc[:, :, ROW0:HW],
                                        op=ALU.add).then_inc(s_vm, 1)
                dve.wait_ge(s_vm, base + 1)
                nc.vector.scalar_tensor_tensor(out=rself[:], in0=zself[:], scalar=SLOPE, in1=zself[:], op0=ALU.mult,
                                               op1=ALU.max).then_inc(s_vm, 1)
                dve.wait_ge(s_vm, base + 2)
                dve.wait_ge(s_mtp, c + 1)
                nc.vector.tensor_tensor(out=zself[:], in0=rself[:], in1=shf, op=ALU.subtract).then_inc(s_mlog, 1)
                dve.wait_ge(s_mp, c + 1)
                nc.vector.tensor_tensor(out=rself[:], in0=pself[:], in1=den, op=ALU.add).then_inc(s_vm, 1)
                nc.vector.tensor_tensor(out=tmp3.rearrange("p b (h c) -> p b h c", h=H),
                                        in0=hwc[:, :, 0:D].rearrange("p b (h c) -> p b h c", h=H),
                                        in1=pself[:].unsqueeze(3).to_broadcast([P, CB, H, C]),
                                        op=ALU.mult).then_inc(s_vm, 1)
                dve.wait_ge(s_vm, base + 4)
                nc.vector.reciprocal(zself[:], rself[:]).then_inc(s_vm, 1)
                nc.vector.tensor_tensor(out=tmp3, in0=tmp3, in1=num, op=ALU.add).then_inc(s_vm, 1)
                dve.wait_ge(s_vm, base + 6)
                nc.vector.tensor_tensor(out=tmp3.rearrange("p b (h c) -> p b h c", h=H),
                                        in0=tmp3.rearrange("p b (h c) -> p b h c", h=H),
                                        in1=zself[:].unsqueeze(3).to_broadcast([P, CB, H, C]),
                                        op=ALU.mult).then_inc(s_vm, 1)
                nc.vector.tensor_tensor(out=xv, in0=xv, in1=bias0_b[:].unsqueeze(1).to_broadcast([P, CB, D]),
                                        op=ALU.add).then_inc(s_vm, 1)
                dve.wait_ge(s_vm, base + 8)
                nc.vector.tensor_tensor(out=xv, in0=xv, in1=tmp3, op=ALU.add).then_inc(s_vm, 1)
                dve.wait_ge(s_vm, base + 9)
                dve.nop(nofuse=True)
                layernorm(c, c + NC)
                dve.wait_ge(s_h1p, c + 1)
                dve.wait_ge(s_tab1, c * 16 + 16)
            nc.vector.memset(big[:], 0.0).then_inc(s_zero, 1)
            dve.wait_ge(s_zero, 1)

            with dve.If(general < 1):
                with dve.Fori(0, NI) as i:
                    for s in range(2):
                        gi = i * 2 + s
                        step = gi * 6
                        nc.vector.tensor_tensor(
                            out=oh[:], in0=typ_f[:, bass.ds(gi * G, G)].unsqueeze(2).to_broadcast([P, G, R]),
                            in1=iota[:].unsqueeze(1).to_broadcast([P, G, R]), op=ALU.is_equal).then_inc(s_oe, 1)
                        nc.vector.tensor_tensor(
                            out=oh1[:], in0=loc1[:, bass.ds(gi * G, G)].unsqueeze(2).to_broadcast([P, G, W1]),
                            in1=iota[:, 0:W1].unsqueeze(1).to_broadcast([P, G, W1]),
                            op=ALU.is_equal).then_inc(s_v1, 1)
                        n0 = [dve.value_load(first[0:1, bass.ds(gi * G + k * S1, 1)], min_val=0, max_val=N)
                              for k in range(G // S1)]
                        dve.wait_ge(s_cop, gi + 1)
                        nc.vector.tensor_tensor(
                            out=coef[:], in0=bank(1, G * B).rearrange("p (t b) -> p t b", t=G),
                            in1=wgt[:, bass.ds(gi * G, G)].unsqueeze(2).to_broadcast([P, G, B]),
                            op=ALU.mult).then_inc(s_v1, 1)
                        dve.wait_ge(s_v1, step + 2)
                        nc.vector.tensor_tensor(
                            out=sel1, in0=oh1[:].unsqueeze(2).to_broadcast([P, G, B, W1]),
                            in1=coef[:].unsqueeze(3).to_broadcast([P, G, B, W1]), op=ALU.mult).then_inc(s_sel, 1)
                        dve.wait_ge(s_agg1, gi + 1)
                        for k in range(G // S1):
                            dve.wait_ge(s_v1, step + 2 + k)
                            table = agg1[:, :, bass.ds(n0[k], W1)]
                            nc.vector.tensor_tensor(
                                out=table, in0=table, in1=bank(2, B * W1, k * B * W1).rearrange("p (b w) -> p b w", b=B),
                                op=ALU.add).then_inc(s_v1, 1)
                dve.wait_ge(s_v1, 12 * NI)
            with dve.If(general > 0):
                with dve.Fori(0, T) as t:
                    nc.vector.tensor_tensor(out=oh[:, 0, :], in0=typ_f[:, bass.ds(t, 1)].to_broadcast([P, R]),
                                            in1=iota[:], op=ALU.is_equal).then_inc(s_oe, 1)
                    dve.wait_ge(s_oep, t + 1)
                    nc.vector.tensor_copy(ohT[0:R, 0, :], bank(0, P)[0:R]).then_inc(s_oeT, 1)
                    dve.wait_ge(s_cop, t + 1)
                    nc.vector.tensor_tensor(out=coef[:, 0, :], in0=bank(1, B),
                                            in1=wgt[:, bass.ds(t, 1)].to_broadcast([P, B]),
                                            op=ALU.mult).then_inc(s_gc, 1)
                    dve.wait_ge(s_gr, t * 16 + 16)
                    dve.nop(nofuse=True)
                    with dve.Fori(0, TILE) as e:
                        u = dve.value_load(src_t[bass.ds(e, 1), bass.ds(t, 1)], min_val=0, max_val=N - 1)
                        v = dve.value_load(dst_t[bass.ds(e, 1), bass.ds(t, 1)], min_val=0, max_val=N)
                        nc.vector.scalar_tensor_tensor(
                            out=agg1[:, :, bass.ds(v, 1)].rearrange("p b o -> p (b o)"), in0=gcb[:, bass.ds(e * B, B)],
                            scalar=h1T[:, bass.ds(u, 1)],
                            in1=agg1[:, :, bass.ds(v, 1)].rearrange("p b o -> p (b o)"), op0=ALU.mult,
                            op1=ALU.add).then_inc(s_gv, 1)
                        dve.wait_ge(s_gv, e + 1)
                        dve.nop(nofuse=True)
                    dve.sem_clear(s_gv)
            nc.vector.memset(mark[:, 2:3], 0.0).then_inc(s_l1, 1)


            for k in range(2):
                nc.vector.memset(mark[:, 3 + k:4 + k], 0.0).then_inc(s_fo, 1)

            def finish(n, s, stores):
                dve.wait_ge(s_fp, n + 3)
                if stores is not None:
                    dve.wait_ge(s_out[s], stores)
                at = bass.ds(n * P, P) if not isinstance(n, int) else slice(n * P, n * P + P)
                nc.vector.scalar_tensor_tensor(out=outc[:, s, :], in0=bank(3 + s, D), scalar=0.0, in1=xs[:, at],
                                               op0=ALU.max, op1=ALU.add).then_inc(s_fo, 1)

            finish(0, 0, None)
            finish(1, 1, None)
            with dve.Fori(1, NB // 2) as i:
                finish(i * 2, 0, i * 16)
                finish(i * 2 + 1, 1, i * 16)
            finish(NB - 1, 0, NB // 2 * 16)

        @block.tensor
        def _(pe):
            mm, tr = nc.tensor.matmul, nc.tensor.transpose

            def cols(at, n, rows=P):
                return ps[0:rows, at:at + n]

            def blocks(src, at):
                for k in range(CB):
                    last = tr(cols(at + k * P, P), src[:, k * P:k * P + P], ident[:])
                return last

            def wide(at, w, rows):
                mm(cols(at, 512, rows), w, hcT[:, 0:512], start=True, stop=True)
                return mm(cols(at + 512, CW - 512, rows), w, hcT[:, 512:CW], start=True, stop=True)

            pe.wait_ge(s_const, 16 * CONST_DMAS)
            pe.wait_ge(s_gset, 3)
            tr(cols(0, P), w_sb[:], ident[:]).then_inc(s_pset, 1)
            pe.wait_ge(s_vset, 10)
            mm(cols(512, 2 * H), wT[:], att_m[:], start=True, stop=True).then_inc(s_pset, 1)
            pe.wait_ge(s_vset, VS)
            with pe.Fori(0, NC) as c:
                pe.wait_ge(s_hc, c + 1)
                blocks(hc, 0).then_inc(s_hcp, 1)
                pe.wait_ge(s_hcT, c + 1)
                for k in range(CB):
                    last = mm(cols(1024 + k * 256, HW), hcT[:, k * P:k * P + P], wcat[:], start=True, stop=True)
                last.then_inc(s_prj, 1)
                wide(5 * 512, w_dd[:], M2)
                wide(0, w_ss[:], M2).then_inc(s_sc, 1)
                pe.wait_ge(s_scc, c + 1)
                wide(5 * 512, w_sb[:], P).then_inc(s_prT, 1)
            pe.wait_ge(s_vset, VS + 13)
            mm(cols(7 * 512, 2, 1), ones[:, 0:1], bad[:, 0:2], start=True, stop=True).then_inc(s_pset, 1)
            pe.wait_ge(s_flag, 1)
            general = pe.value_load(flag[0:1, 0:1], min_val=0, max_val=1)

            with pe.If(general < 1):
                with pe.Fori(0, NI) as i:
                    for s in range(2):
                        gi = i * 2 + s
                        pe.wait_ge(s_oh, gi + 1)
                        for k in range(2):
                            last = tr(cols(k * P, P), oh[:, k * S0:k * S0 + S0, :].rearrange("p t w -> p (t w)"), ident[:])
                        last.then_inc(s_ohp, 1)
                        pe.wait_ge(s_awin, gi + 1)
                        for k in range(2):
                            last = mm(cols(512 + k * 2 * H, 2 * H), awin[:, k].rearrange("p q w -> p (q w)"), pick[:],
                                      start=True, stop=True)
                        last.then_inc(s_winp, 1)
                        pe.wait_ge(s_ohT, gi + 1)
                        pe.wait_ge(s_bdw, gi + 1)
                        for k in range(2):
                            last = mm(cols(1024 + k * 8 * H, 8 * H), ohT[:, k, :],
                                      bdw[:, k].rearrange("p q h -> p (q h)"), start=True, stop=True)
                        last.then_inc(s_ade, 1)
                        pe.wait_ge(s_msg, gi + 1)
                        for k in range(2):
                            for j in range(S0):
                                t = k * S0 + j
                                mm(cols(3 * 512 + k * W0, W0), msg[:, t, :], oh[:, t, :], start=(j == 0),
                                   stop=(j == S0 - 1))
                            for j in range(S0):
                                t = k * S0 + j
                                last = mm(cols(4 * 512 + k * W0, W0, H), pt[:, t, :], oh[:, t, :], start=(j == 0),
                                          stop=(j == S0 - 1))
                        last.then_inc(s_agg, 1)
            with pe.If(general > 0):
                with pe.Fori(0, T) as t:
                    pe.wait_ge(s_gp, t + 1)
                    mm(cols(0, TILE), head_to[:], gp, start=True, stop=True).then_inc(s_gb, 1)

            with pe.Fori(0, NC) as c:
                pe.wait_ge(s_mst, c * 3 + 3)
                blocks(stg, 4 * 512)
                for k in range(CB):
                    at = slice(k * P, k * P + P)
                    tr(cols(3 * 512 + k * H, H), dstg[:, at], ident[0:H, 0:H])
                    last = tr(cols(2 * 512 + k * H, H), mstg[32:M2, at], ident[32:M2, 32:M2])
                last.then_inc(s_mtp, 1)
                pe.wait_ge(s_hc, c + NC + 1)
                blocks(hc, 0).then_inc(s_h1p, 1)
            pe.wait_ge(s_h1T, NC)

            with pe.If(general < 1):
                with pe.Fori(0, NI) as i:
                    for s in range(2):
                        gi = i * 2 + s
                        pe.wait_ge(s_oe, gi + 1)
                        for k in range(2):
                            last = tr(cols(k * P, P), oh[:, k * 4:k * 4 + 4, :].rearrange("p t w -> p (t w)"), ident[:])
                        last.then_inc(s_oep, 1)
                        pe.wait_ge(s_oeT, gi + 1)
                        for k in range(2):
                            last = mm(cols(512 + k * 4 * B, 4 * B), ohT[:, k, :],
                                      comp_bd[:].rearrange("p q b -> p (q b)"), start=True, stop=True)
                        last.then_inc(s_cop, 1)
                        pe.wait_ge(s_sel, gi + 1)
                        pe.wait_ge(got1[s], i * (16 * G) + 16 * G)
                        for t in range(G):
                            last = mm(cols(2 * 512 + t // S1 * B * W1, B * W1), g1[:, s, t, :],
                                      sel1[:, t].rearrange("p b w -> p (b w)"), start=(t % S1 == 0),
                                      stop=(t % S1 == S1 - 1))
                        last.then_inc(s_agg1, 1)
            with pe.If(general > 0):
                with pe.Fori(0, T) as t:
                    pe.wait_ge(s_oe, t + 1)
                    tr(cols(0, P, R), oh[:, 0, :], ident[:]).then_inc(s_oep, 1)
                    pe.wait_ge(s_oeT, t + 1)
                    mm(cols(512, B), ohT[0:R, 0, :], comp4[0:R, :], start=True, stop=True).then_inc(s_cop, 1)

            for _ in range(2):
                pe.sem_inc(s_fp, 1)

            def product(n, s):
                pe.wait_ge(s_fst, n * 2 + 2)
                pe.wait_ge(s_fo, n + 1)
                for b in range(B):
                    mm(cols((3 + s) * 512, D), aggc[:, s, b, :], basis_sb[:, b, :], start=(b == 0), stop=False)
                mm(cols((3 + s) * 512, D), h1c[:, s, :], loop_sb[:], start=False, stop=False)
                mm(cols((3 + s) * 512, D), ones[0:1, :], bias1_b[0:1, :], start=False, stop=True).then_inc(s_fp, 1)

            with pe.Fori(0, NB // 2) as i:
                product(i * 2, 0)
                product(i * 2 + 1, 1)
            product(NB - 1, 0)


def kernel(x, src, dst, edge_type_32, edge_weight1, L0_gnn_W, L0_gnn_att_src, L0_gnn_att_dst, L0_gnn_bias,
           L1_gnn_weight, L1_gnn_w_comp, L1_gnn_loop_weight, L1_gnn_h_bias):
    import numpy as np
    import concourse.bacc as bacc
    from concourse.bass_utils import run_bass_kernel_spmd

    def tiles(a, pad, n):
        full = np.full(n * TILE, pad, a.dtype)
        full[:E] = a.reshape(-1)
        return np.ascontiguousarray(full.reshape(n, TILE).T)

    xp = np.zeros((NP, D), x.dtype)
    xp[:N] = x
    arrays = {
        "x_pad": xp, "src_t": tiles(src, 0, T + 2 * G), "dst_t": tiles(dst, N, T),
        "typ_t": tiles(edge_type_32, 0, T), "wgt_t": tiles(edge_weight1, 0, T), "w_att": L0_gnn_W,
        "att_src": L0_gnn_att_src, "att_dst": L0_gnn_att_dst, "bias0": L0_gnn_bias, "basis": L1_gnn_weight,
        "w_comp": L1_gnn_w_comp, "w_loop": L1_gnn_loop_weight, "bias1": L1_gnn_h_bias,
    }
    nc = bacc.Bacc("TRN2", target_bir_lowering=False, num_devices=1)
    arrays = {k: np.ascontiguousarray(v) for k, v in arrays.items()}
    args = [nc.dram_tensor(k, v.shape, mybir.dt.from_np(v.dtype), kind="ExternalInput").ap()
            for k, v in arrays.items()]
    out = nc.dram_tensor("out", (NP, D), mybir.dt.float32, kind="ExternalOutput").ap()
    build(nc, *args, out)
    res = run_bass_kernel_spmd(nc, [arrays], core_ids=[0])
    return res.results[0]["out"][:N]
```

```python
from contextlib import ExitStack

import concourse.bass as bass
from concourse import mybir

P = 128
N, E, D, H, C, R, B = 3125, 103125, 128, 8, 16, 32, 8
TILE = 128
G = 8
SL = 4
NG = -(-(E - TILE * G) // (TILE * G * SL)) * SL + 1
T = NG * G
TT = T + SL * G
NI = (NG - 1) // SL
W0, S0 = 32, 4
W1, S1 = 16, 2
NB = -(-N // P)
NP = NB * P
CB = 5
NC = NB // CB
CW = CB * P
ROW0 = D + H
HW = D + 2 * H
SPREAD = 60.0
EPS = 1e-5
SLOPE = 0.2
VS = 14
M2 = 32 + H


def build(nc, x, src_t, dst_t, typ_t, wgt_t, w_att, att_src, att_dst, bias0, basis,
          w_comp, w_loop, bias1, out):
    f32, i32 = mybir.dt.float32, mybir.dt.int32
    ALU, ACT, AX = mybir.AluOpType, mybir.ActivationFunctionType, mybir.AxisListType
    ctx = ExitStack()
    with ctx:
        def sb(name, shape, dt=f32):
            return ctx.enter_context(nc.sbuf_tensor(name, shape, dt))

        def sem(name):
            return ctx.enter_context(nc.semaphore(name))

        table0 = nc.dram_tensor("table0", (NP, ROW0), f32, kind="Internal").ap()
        table1 = nc.dram_tensor("table1", (NP, D), f32, kind="Internal").ap()
        coef_row = nc.dram_tensor("coef_row", (TILE, B), f32, kind="Internal").ap()

        src_i = sb("src_i", [P, TT], i32)
        loc0 = sb("loc0", [P, TT])
        loc1 = sb("loc1", [P, TT])
        typ_f = sb("typ_f", [P, TT])
        wgt = sb("wgt", [P, TT])
        xs = sb("xs", [P, NB * D])
        h1T = sb("h1T", [P, NP])
        hl = sb("hl", [P, NP])
        big = sb("big", [P, B * NP])
        agg1 = big[:, :].rearrange("p (b n) -> p b n", b=B)
        aggT = big[:, 0:NP]
        denT = big[:, NP:2 * NP]
        winT = big[:, 2 * NP:3 * NP]
        dscT = big[:, 3 * NP:4 * NP]
        sscT = big[:, 4 * NP:5 * NP]
        maxT = big[:, 5 * NP:6 * NP]
        hw = big[:, 6 * NP:6 * NP + NB * HW].rearrange("p (b f) -> p b f", b=NB)

        ones = sb("ones", [P, P])
        ident = sb("ident", [P, P])
        iota_i = sb("iota_i", [P, W0], i32)
        iota = sb("iota", [P, W0])
        quad = sb("quad", [P, 4])
        head_of = sb("head_of", [P, H])
        head_to = sb("head_to", [H, P])
        pick = sb("pick", [M2, 2 * H])
        w_sb = sb("w_sb", [P, D])
        wT = sb("wT", [P, D])
        att_c = sb("att_c", [P, 2])
        att_m = sb("att_m", [P, 2 * H])
        wcat = sb("wcat", [P, HW])
        w_sc = sb("w_sc", [P, 64 + M2])
        comp4 = sb("comp4", [P, B])
        comp_bd = sb("comp_bd", [P, 4, B])
        basis_sb = sb("basis_sb", [P, B, D])
        loop_sb = sb("loop_sb", [P, D])
        bias0_b = sb("bias0_b", [P, D])
        bias1_b = sb("bias1_b", [P, D])
        eps_t = sb("eps_t", [P, 1])
        smax = sb("smax", [M2, 1])
        smin = sb("smin", [M2, 1])
        bad = sb("bad", [P, 4])
        mark = sb("mark", [P, 6])
        flag_f = sb("flag_f", [1, 1])
        flag = sb("flag", [1, 1], i32)
        stats = sb("stats", [P, CB, 6])
        mv = sb("mv", [P, CB, 2])
        nmr = sb("nmr", [P, CB])
        smc = sb("smc", [M2, 2, NC])
        rinv = sb("rinv", [P, CB])
        rstd = sb("rstd", [P, CB])

        work = sb("work", [P, SL * G * ROW0 + 3 * G * D])
        GW = SL * G * ROW0
        g0 = work[:, 0:GW].rearrange("p (s t f) -> p s t f", s=SL, t=G)
        msg = work[:, GW:GW + 2 * G * D].rearrange("p (s t f) -> p s t f", s=2, t=G)
        g1 = work[:, 0:SL * G * D].rearrange("p (s t f) -> p s t f", s=SL, t=G)
        sel1 = work[:, GW:GW + 2 * G * D].rearrange("p (s t b w) -> p s t b w", s=2, t=G, b=B)
        hc = work[:, 0:2 * CW].rearrange("p (s f) -> p s f", s=2)
        hcT = work[:, 2 * CW:3 * CW]
        tmp3 = work[:, 3 * CW:4 * CW].rearrange("p (b f) -> p b f", b=CB)
        stg = work[:, 4 * CW:5 * CW]
        dstg = work[0:H, 5 * CW:6 * CW]
        basei = big[:, 5 * NP:5 * NP + TT].bitcast(i32)
        dst_i = big[:, 5 * NP + TT:5 * NP + 2 * TT].bitcast(i32)
        typ_i = big[:, 5 * NP + 2 * TT:5 * NP + 3 * TT].bitcast(i32)
        chk = big[:, 6 * NP + NB * HW:6 * NP + NB * HW + TT]
        dst_f = hl[:, TT:2 * TT]
        base_f, clip0, clip1, real = (h1T[:, k * TT:k * TT + TT] if k < 3 else hl[:, 0:TT] for k in range(4))
        gz, gm, gp = (work[0:H, k * TILE:k * TILE + TILE] for k in range(3))
        hwT = work[:, GW + 3 * G * D - NP:GW + 3 * G * D]
        gcb = work[:, GW:GW + TILE * B]
        aggc = work[:, 0:2 * B * P].rearrange("p (s b n) -> p s b n", s=2, b=B)
        pre = work[:, 2 * B * P:2 * B * P + 2 * P].rearrange("p (s n) -> p s n", s=2)
        outc = work[:, 2 * B * P + 2 * P:2 * B * P + 4 * P].rearrange("p (s n) -> p s n", s=2)

        first = sb("first", [1, TT], i32)
        idx = sb("idx", [P, SL, G], i32)
        oh = sb("oh", [P, SL, G, W0])
        ohT = sb("ohT", [P, 2, P])
        awin = sb("awin", [M2, 2, 4, W0])
        bdw = sb("bdw", [P, 2, 4, 2 * H])
        zt = sb("zt", [P, G, H])
        lt = sb("lt", [P, G, H])
        pt = sb("pt", [P, 2, G, H])
        oh1 = sb("oh1", [P, G, W1])
        coef = sb("coef", [P, G, B])
        pself = sb("pself", [P, NB, H])
        zself = sb("zself", [P, NB, H])
        lself = sb("lself", [P, NB, H])
        den_s = sb("den_s", [P, CB, H])
        rden = sb("rden", [P, CB, H])

        ps = ctx.enter_context(nc.psum_tensor("ps", [P, 8 * 512], f32))

        def at(start, size):
            return slice(start, start + size) if isinstance(start, int) else bass.ds(start, size)

        def bank(k, cols, off=0):
            return ps[:, k * 512 + off:k * 512 + off + cols]

        s_const = sem("s_const")
        s_edges = sem("s_edges")
        s_x = sem("s_x")
        s_src = sem("s_src")
        s_gset = sem("s_gset")
        s_vset = sem("s_vset")
        s_pset = sem("s_pset")
        s_gt0 = sem("s_gt0")
        s_test = sem("s_test")
        s_flag = sem("s_flag")
        s_hc = sem("s_hc")
        s_sqrt = sem("s_sqrt")
        s_var = sem("s_var")
        s_hcp = sem("s_hcp")
        s_hcT = sem("s_hcT")
        s_prj = sem("s_prj")
        s_prjc = sem("s_prjc")
        s_sc = sem("s_sc")
        s_scc = sem("s_scc")
        s_tab0 = sem("s_tab0")
        s_prep = sem("s_prep")
        got0 = [sem(f"got0_{s}") for s in range(SL)]
        got1 = [sem(f"got1_{s}") for s in range(SL)]
        s_idx = sem("s_idx")
        s_oh = sem("s_oh")
        s_ohp = sem("s_ohp")
        s_ohT = sem("s_ohT")
        s_awin = sem("s_awin")
        s_winp = sem("s_winp")
        s_bdw = sem("s_bdw")
        s_ade = sem("s_ade")
        s_log = sem("s_log")
        s_p = sem("s_p")
        s_msg = sem("s_msg")
        s_agg = sem("s_agg")
        s_v0 = sem("s_v0")
        s_a0 = sem("s_a0")
        s_l0 = sem("s_l0")
        s_idx1 = sem("s_idx1")
        s_oe = sem("s_oe")
        s_oep = sem("s_oep")
        s_oeT = sem("s_oeT")
        s_cop = sem("s_cop")
        s_sel = sem("s_sel")
        s_agg1 = sem("s_agg1")
        s_a1 = sem("s_a1")
        s_v1 = sem("s_v1")
        s_l1 = sem("s_l1")
        s_nmr = sem("s_nmr")
        s_self = sem("s_self")
        s_slog = sem("s_slog")
        s_sp = sem("s_sp")
        s_sv = sem("s_sv")
        s_mst = sem("s_mst")
        s_mtp = sem("s_mtp")
        s_vm = sem("s_vm")
        s_vs = sem("s_vs")
        s_h1p = sem("s_h1p")
        s_h1T = sem("s_h1T")
        s_hlp = sem("s_hlp")
        s_hl = sem("s_hl")
        s_hfree = sem("s_hfree")
        s_tab1 = sem("s_tab1")
        s_zero = sem("s_zero")
        s_fst = sem("s_fst")
        s_fp = sem("s_fp")
        s_fv = sem("s_fv")
        s_fo = sem("s_fo")
        s_out = [sem("s_out_a"), sem("s_out_b")]
        s_gv = sem("s_gv")
        s_gst = sem("s_gst")
        s_gt = sem("s_gt")
        s_ghw = sem("s_ghw")
        s_gz = sem("s_gz")
        s_gp = sem("s_gp")
        s_gb = sem("s_gb")
        s_gc = sem("s_gc")
        s_gw = sem("s_gw")
        s_gr = sem("s_gr")
        s_gu = sem("s_gu")

        block = ctx.enter_context(nc.Block())

        def ade(par):
            return bank(7 if par else 2, 2 * 4 * 2 * H)

        def pairs(eng, step):
            with eng.Fori(0, NC // 2) as i:
                step(i * 2, 0)
                step(i * 2 + 1, 1)
            step(NC - 1, 0)

        def last_chunk(c):
            return isinstance(c, int) and c == NC - 1

        def groups(eng, step):
            step(0, 0, 1)
            with eng.Fori(0, NI) as i:
                for k in range(1, SL + 1):
                    step(i * SL + k, k % SL, i + 1 + k // SL)
        CONST_DMAS = 11
        EDGE_DMAS = 5

        @block.sync
        def _(sp):
            sp.dma_start(xs[:, :].rearrange("p (b f) -> p b f", b=NB),
                         x.rearrange("(b p) f -> p b f", p=P)).then_inc(s_x, 16)
            sp.dma_start(w_sb[:], w_att).then_inc(s_const, 16)
            sp.dma_start(att_c[:, 0:1], att_src.rearrange("h (c o) -> (h c) o", o=1)).then_inc(s_const, 16)
            sp.dma_start(att_c[:, 1:2], att_dst.rearrange("h (c o) -> (h c) o", o=1)).then_inc(s_const, 16)
            sp.dma_start(src_i[:], src_t).then_inc(s_src, 16)
            sp.dma_start(dst_i, dst_t).then_inc(s_edges, 16)
            sp.dma_start(basei, dst_t[0, :].partition_broadcast(P)).then_inc(s_edges, 16)
            sp.dma_start(first[:], dst_t[0:1, :]).then_inc(s_edges, 16)
            sp.dma_start(typ_i, typ_t).then_inc(s_edges, 16)
            sp.dma_start(wgt[:], wgt_t).then_inc(s_edges, 16)
            for q in range(4):
                sp.dma_start(comp4[32 * q:32 * q + R, :], w_comp).then_inc(s_const, 16)
            sp.dma_start(basis_sb[:], basis.rearrange("b d f -> d b f")).then_inc(s_const, 16)
            sp.dma_start(loop_sb[:], w_loop).then_inc(s_const, 16)
            sp.dma_start(bias0_b[:], bias0.partition_broadcast(P)).then_inc(s_const, 16)
            sp.dma_start(bias1_b[:], bias1.partition_broadcast(P)).then_inc(s_const, 16)
            with sp.Fori(0, NC) as c:
                sp.wait_ge(s_prjc, c + 1)
                sp.dma_start(table0[bass.ds(c * CW, CW), :].rearrange("(b p) f -> p b f", p=P),
                             hw[:, bass.ds(c * CB, CB), 0:ROW0]).then_inc(s_tab0, 16)
            sp.sem_inc(s_hfree, 2)

            def store_h1(c, s):
                sp.wait_ge(s_hc, c + NC + 1)
                sp.dma_start(table1[at(c * CW, CW), :].rearrange("(b p) f -> p b f", p=P),
                             hc[:, s].rearrange("p (b f) -> p b f", b=CB)).then_inc(s_tab1, 16)
                sp.wait_ge(s_tab1, c * 16 + 16)
                sp.sem_inc(s_hfree, 1)

            pairs(sp, store_h1)
            sp.wait_ge(s_flag, 1)
            general = sp.value_load(flag[0:1, 0:1], min_val=0, max_val=1)
            with sp.If(general > 0):
                with sp.Fori(0, T) as t:
                    sp.wait_ge(s_gc, t + 1)
                    sp.dma_start(coef_row, coef[:, 0, :]).then_inc(s_gw, 16)
                    sp.wait_ge(s_gw, t * 16 + 16)
                    sp.dma_start(gcb,
                                 coef_row.rearrange("(o e) b -> o (e b)", o=1)[0].partition_broadcast(P)
                                 ).then_inc(s_gr, 16)

            def store(n, s):
                sp.wait_ge(s_fo, n + 3)
                sp.dma_start(out[at(n * P, P), :],
                             outc[:, s, :]).then_inc(s_out[s], 16)

            with sp.Fori(0, NB // 2) as i:
                store(i * 2, 0)
                store(i * 2 + 1, 1)
            store(NB - 1, 0)
            sp.wait_ge(s_out[0], 16 * (NB // 2 + 1))
            sp.wait_ge(s_out[1], 16 * (NB // 2))

        @block.gpsimd
        def _(pool):
            nc.gpsimd.iota(iota_i[:], pattern=[[1, W0]], base=0, channel_multiplier=0).then_inc(s_gset, 1)
            nc.gpsimd.memset(ones[:], 1.0).then_inc(s_gset, 1)
            pool.wait_ge(s_gset, 2)
            nc.gpsimd.affine_select(out=ident[:], in_=ones[:], pattern=[[-1, P]], base=0, channel_multiplier=1,
                                    compare_op=ALU.is_equal, fill=0.0).then_inc(s_gset, 1)
            nc.gpsimd.affine_select(out=quad[:], in_=ones[:, 0:4], pattern=[[-32, 4]], base=0,
                                    channel_multiplier=1, compare_op=ALU.is_ge, fill=0.0).then_inc(s_gset, 1)
            nc.gpsimd.affine_select(out=head_of[:], in_=ones[:, 0:H], pattern=[[-C, H]], base=0,
                                    channel_multiplier=1, compare_op=ALU.is_ge, fill=0.0).then_inc(s_gset, 1)
            nc.gpsimd.affine_select(out=head_to[:], in_=ones[0:H, :], pattern=[[1, P]], base=0,
                                    channel_multiplier=-C, compare_op=ALU.is_ge, fill=0.0).then_inc(s_gset, 1)
            nc.gpsimd.affine_select(out=pick[:, 0:H], in_=ones[0:M2, 0:H], pattern=[[-1, H]], base=0,
                                    channel_multiplier=1, compare_op=ALU.is_equal, fill=0.0).then_inc(s_gset, 1)
            nc.gpsimd.affine_select(out=pick[:, H:2 * H], in_=ones[0:M2, 0:H], pattern=[[-1, H]], base=-32,
                                    channel_multiplier=1, compare_op=ALU.is_equal, fill=0.0).then_inc(s_gset, 1)
            pool.wait_ge(s_gset, 8)
            nc.gpsimd.affine_select(out=quad[:], in_=quad[:], pattern=[[32, 4]], base=31,
                                    channel_multiplier=-1, compare_op=ALU.is_ge, fill=0.0).then_inc(s_gset, 1)
            nc.gpsimd.affine_select(out=head_of[:], in_=head_of[:], pattern=[[C, H]], base=C - 1,
                                    channel_multiplier=-1, compare_op=ALU.is_ge, fill=0.0).then_inc(s_gset, 1)
            nc.gpsimd.affine_select(out=head_to[:], in_=head_to[:], pattern=[[-1, P]], base=C - 1,
                                    channel_multiplier=C, compare_op=ALU.is_ge, fill=0.0).then_inc(s_gset, 1)
            nc.gpsimd.memset(aggT, 0.0).then_inc(s_gset, 1)
            nc.gpsimd.memset(denT[0:H], 0.0).then_inc(s_gset, 1)
            nc.gpsimd.memset(winT[0:M2], 0.0).then_inc(s_gset, 1)

            pool.wait_ge(s_edges, 16 * EDGE_DMAS)
            nc.gpsimd.tensor_copy(dst_f, dst_i).then_inc(s_gt0, 1)
            nc.gpsimd.tensor_copy(base_f, basei).then_inc(s_gt0, 1)
            nc.gpsimd.tensor_copy(typ_f[:], typ_i).then_inc(s_gt0, 1)
            pool.wait_ge(s_gt0, 2)
            for loc, sh in ((loc0, S0), (loc1, S1)):
                nc.gpsimd.tensor_tensor(
                    out=loc[:].rearrange("p (k j) -> p k j", j=sh), in0=dst_f.rearrange("p (k j) -> p k j", j=sh),
                    in1=base_f.rearrange("p (k j) -> p k j", j=sh)[:, :, 0:1].to_broadcast([P, TT // sh, sh]),
                    op=ALU.subtract).then_inc(s_gt0, 1)
            step = 5
            for loc, width, clipped in ((loc0, W0, clip0), (loc1, W1, clip1)):
                pool.wait_ge(s_gt0, step)
                nc.gpsimd.tensor_scalar(out=clipped, in0=loc[:], scalar1=0.0, scalar2=width - 1.0, op0=ALU.max,
                                        op1=ALU.min).then_inc(s_gt0, 1)
                pool.wait_ge(s_gt0, step + 1)
                nc.gpsimd.tensor_tensor(out=clipped, in0=clipped, in1=loc[:], op=ALU.subtract).then_inc(s_gt0, 1)
                pool.wait_ge(s_gt0, step + 2)
                nc.gpsimd.tensor_tensor(out=clipped, in0=clipped, in1=clipped, op=ALU.mult).then_inc(s_gt0, 1)
                step += 3
            nc.gpsimd.tensor_scalar(out=real, in0=dst_f, scalar1=float(N), scalar2=None,
                                    op0=ALU.is_lt).then_inc(s_gt0, 1)
            pool.wait_ge(s_gt0, 12)
            nc.gpsimd.tensor_tensor(out=clip0, in0=clip0, in1=clip1, op=ALU.add).then_inc(s_gt0, 1)
            pool.wait_ge(s_gt0, 13)
            nc.gpsimd.tensor_tensor(out=chk, in0=clip0, in1=real, op=ALU.mult).then_inc(s_test, 1)

            pool.wait_ge(s_flag, 1)
            general = pool.value_load(flag[0:1, 0:1], min_val=0, max_val=1)

            def gathers(table, g, got, staged):
                def step(gi, s, nth):
                    pool.wait_ge(staged, gi + 1)
                    pool.nop(nofuse=True)
                    for t in range(G):
                        nc.gpsimd.indirect_dma_start(
                            out=g[:, s, t, :], out_offset=None, in_=table,
                            in_offset=bass.IndirectOffsetOnAxis(ap=idx[:, s, t:t + 1], axis=0),
                        ).then_inc(got[s], 16)
                groups(pool, step)

            pool.wait_ge(s_tab0, 16 * NC)
            with pool.If(general < 1):
                gathers(table0, g0, got0, s_idx)
            pool.wait_ge(s_tab1, 16 * NC)
            with pool.If(general < 1):
                gathers(table1, g1, got1, s_idx1)

        @block.scalar
        def _(act):
            def root(chunk):
                act.wait_ge(s_var, chunk + 1)
                nc.scalar.activation(rstd[:], mv[:, :, 1], ACT.Sqrt, bias=eps_t[:], scale=1.0).then_inc(s_sqrt, 1)

            def normalise(chunk, c, s):
                act.wait_ge(s_nmr, chunk + 1)
                for k in range(CB):
                    last = nc.scalar.activation(hc[:, s, k * D:k * D + D], xs[:, at(c * CW + k * D, D)], ACT.Relu,
                                                bias=nmr[:, k:k + 1], scale=rinv[:, k:k + 1])
                last.then_inc(s_hc, 1)

            def prepare(c, s):
                normalise(c, c, s)
                act.wait_ge(s_hcp, c + 1)
                nc.scalar.copy(hcT, bank(0, CW)).then_inc(s_hcT, 1)
                if not last_chunk(c):
                    root(c + 1)
                act.wait_ge(s_prj, c + 1)
                nc.scalar.copy(hw[:, at(c * CB, CB), :],
                               ps[:, 1024:1024 + CB * 256].rearrange("p (b f) -> p b f", b=CB)[:, :, 0:HW]
                               ).then_inc(s_prjc, 1)

            act.wait_ge(s_vset, 1)
            act.wait_ge(s_x, 16)
            root(0)
            pairs(act, prepare)
            act.wait_ge(s_src, 16)
            act.wait_ge(s_flag, 1)
            general = act.value_load(flag[0:1, 0:1], min_val=0, max_val=1)

            def stage(gi, s, staged):
                nc.scalar.copy(idx[:, s, :], src_i[:, at(gi * G, G)]).then_inc(staged, 1)

            with act.If(general < 1):
                for k in range(SL):
                    stage(k, k, s_idx)
            with act.If(general > 0):
                with act.Fori(0, NC) as c:
                    nc.scalar.copy(stg.rearrange("p (b f) -> p b f", b=CB),
                                   hw[:, bass.ds(c * CB, CB), 0:D]).then_inc(s_gst, 1)
                    act.wait_ge(s_gt, c + 1)
                    nc.scalar.copy(hwT[:, bass.ds(c * CW, CW)], bank(0, CW)).then_inc(s_ghw, 1)
            act.wait_ge(s_slog, 1)
            nc.scalar.activation(pself[:], zself[:], ACT.Exp).then_inc(s_sp, 1)

            def windows(gi):
                for k in range(2):
                    n0 = act.value_load(first[0:1, at(gi * G + k * S0, 1)], min_val=0, max_val=N)
                    last = nc.scalar.copy(awin[:, k, :, :],
                                          winT[0:M2, bass.ds(n0, W0)].unsqueeze(1).to_broadcast([M2, 4, W0]))
                last.then_inc(s_awin, 1)

            def transposed(gi, ready, done):
                act.wait_ge(ready, gi + 1)
                nc.scalar.copy(ohT[:].rearrange("p s e -> p (s e)"), bank(0, 2 * P)).then_inc(done, 1)

            def attention(gi, s, nth):
                transposed(gi + 1, s_ohp, s_ohT)
                act.wait_ge(s_log, gi + 1)
                nc.scalar.activation(pt[:, s % 2], zt[:], ACT.Exp).then_inc(s_p, 1)
                act.wait_ge(s_winp, gi + 2)
                windows(gi + 2)
                act.wait_ge(s_msg, gi + 1)
                stage(gi + SL, s, s_idx)

            with act.If(general < 1):
                act.wait_ge(s_prep, 1)
                windows(0)
                transposed(0, s_ohp, s_ohT)
                act.wait_ge(s_winp, 1)
                windows(1)
                groups(act, attention)
            with act.If(general > 0):
                with act.Fori(0, T) as t:
                    act.wait_ge(s_gz, t + 1)
                    nc.scalar.activation(gp, gz, ACT.Exp).then_inc(s_gp, 1)
            act.wait_ge(s_l0, 1)

            def stage_sums(c):
                nc.scalar.copy(stg, aggT[:, at(c * CW, CW)]).then_inc(s_mst, 1)
                nc.scalar.copy(dstg, denT[0:H, at(c * CW, CW)]).then_inc(s_mst, 1)

            def second(c, s):
                root(c + NC)
                if not last_chunk(c):
                    act.wait_ge(s_mtp, c + 1)
                    stage_sums(c + 1)
                act.wait_ge(s_hfree, c + 1)
                normalise(c + NC, c, s)
                act.wait_ge(s_h1p, c + 1)
                nc.scalar.copy(hcT, bank(0, CW)).then_inc(s_h1T, 1)
                nc.scalar.copy(h1T[:, at(c * CW, CW)], bank(0, CW)).then_inc(s_h1T, 1)
                act.wait_ge(s_hlp, c + 1)
                nc.scalar.copy(hl[:, at(c * CW, CW)], bank(6, CW)).then_inc(s_hl, 1)

            stage_sums(0)
            pairs(act, second)

            def relational(gi, s, nth):
                transposed(gi + 1, s_oep, s_oeT)
                act.wait_ge(s_agg1, gi + 1)
                stage(gi + SL, s, s_idx1)

            with act.If(general < 1):
                for k in range(SL):
                    stage(k, k, s_idx1)
                transposed(0, s_oep, s_oeT)
                groups(act, relational)
            act.wait_ge(s_l1, 1)

            def stage_block(n, s):
                act.wait_ge(s_fp, n + 1)
                nc.scalar.copy(aggc[:, s], agg1[:, :, at(n * P, P)]).then_inc(s_fst, 1)

            with act.Fori(0, NB // 2) as i:
                stage_block(i * 2, 0)
                stage_block(i * 2 + 1, 1)
            stage_block(NB - 1, 0)

        @block.vector
        def _(dve):
            def statistics(chunk, c):
                for k in range(CB):
                    last = nc.vector.bn_stats(out=stats[:, k, :], in_=xs[:, at(c * CW + k * D, D)])
                last.then_inc(s_vs, 1)
                dve.wait_ge(s_vs, chunk * 2 + 1)
                dve.nop(nofuse=True)
                for k in range(CB):
                    last = nc.vector.bn_aggr(out=mv[:, k, :], in_=stats[:, k, :])
                last.then_inc(s_var, 1)

            def scales(chunk):
                dve.wait_ge(s_sqrt, chunk + 1)
                if not isinstance(chunk, int) or chunk:
                    dve.wait_ge(s_hc, chunk)
                nc.vector.reciprocal(rinv[:], rstd[:]).then_inc(s_vs, 1)
                dve.wait_ge(s_vs, chunk * 2 + 2)
                nc.vector.scalar_tensor_tensor(out=nmr[:], in0=mv[:, :, 0], scalar=-1.0, in1=rinv[:], op0=ALU.mult,
                                               op1=ALU.mult).then_inc(s_nmr, 1)

            nc.vector.memset(eps_t[:], EPS).then_inc(s_vset, 1)
            nc.vector.memset(w_sc[:], 0.0).then_inc(s_vset, 1)
            nc.vector.memset(mark[:, 1:2], 0.0).then_inc(s_scc, 1)
            nc.vector.memset(bad[:], 0.0).then_inc(s_vset, 1)
            dve.wait_ge(s_x, 16)
            statistics(0, 0)
            scales(0)
            dve.wait_ge(s_gset, 14)
            dve.wait_ge(s_const, 16 * CONST_DMAS)
            nc.vector.tensor_copy(iota[:], iota_i[:]).then_inc(s_vset, 1)
            for k in range(2):
                nc.vector.tensor_tensor(out=att_m[:, k * H:k * H + H], in0=head_of[:],
                                        in1=att_c[:, k:k + 1].to_broadcast([P, H]), op=ALU.mult).then_inc(s_vset, 1)
            nc.vector.tensor_tensor(out=comp_bd[:], in0=quad[:].unsqueeze(2).to_broadcast([P, 4, B]),
                                    in1=comp4[:].unsqueeze(1).to_broadcast([P, 4, B]), op=ALU.mult).then_inc(s_vset, 1)
            nc.vector.tensor_copy(wcat[:, 0:D], w_sb[:]).then_inc(s_vset, 1)
            dve.wait_ge(s_pset, 1)
            nc.vector.tensor_copy(wT[:], bank(0, P)).then_inc(s_vset, 1)
            dve.wait_ge(s_pset, 2)
            nc.vector.tensor_copy(wcat[:, D:HW], bank(1, 2 * H)).then_inc(s_vset, 1)
            for k in (0, 32):
                nc.vector.tensor_copy(w_sc[:, k:k + H], bank(1, H, H)).then_inc(s_vset, 1)
                nc.vector.tensor_copy(w_sc[:, 64 + k:64 + k + H], bank(1, H)).then_inc(s_vset, 1)

            def prepare(c, s):
                if not last_chunk(c):
                    statistics(c + 1, c + 1)
                    scales(c + 1)
                dve.wait_ge(s_sc, c + 1)
                scores = bank(5, CW)
                nc.vector.tensor_reduce(out=smc[:, 0, at(c, 1)], in_=scores[64:64 + M2], axis=AX.X, op=ALU.max)
                nc.vector.tensor_reduce(out=smc[:, 1, at(c, 1)], in_=scores[64:64 + M2], axis=AX.X, op=ALU.min)
                nc.vector.tensor_copy(dscT[0:M2, at(c * CW, CW)], scores[0:M2])
                nc.vector.tensor_copy(sscT[0:M2, at(c * CW, CW)], scores[64:64 + M2]).then_inc(s_scc, 1)

            pairs(dve, prepare)

            dve.wait_ge(s_scc, NC + 1)
            nc.vector.tensor_reduce(out=smax[:], in_=smc[:, 0, :], axis=AX.X, op=ALU.max).then_inc(s_vset, 1)
            nc.vector.tensor_reduce(out=smin[:], in_=smc[:, 1, :], axis=AX.X, op=ALU.min).then_inc(s_vset, 1)
            dve.wait_ge(s_test, 1)
            nc.vector.tensor_reduce(out=bad[:, 0:1], in_=chk, axis=AX.X, op=ALU.max).then_inc(s_vset, 1)
            dve.wait_ge(s_vset, VS + 3)
            nc.vector.tensor_scalar(out=bad[0:H, 1:2], in0=smax[0:H], scalar1=smin[0:H], scalar2=SPREAD,
                                    op0=ALU.subtract, op1=ALU.is_gt).then_inc(s_vset, 1)
            dve.wait_ge(s_pset, 3)
            nc.vector.tensor_reduce(out=flag_f[:], in_=bank(7, 2)[0:1], axis=AX.X, op=ALU.add).then_inc(s_vset, 1)
            dve.wait_ge(s_vset, VS + 5)
            nc.vector.tensor_scalar(out=flag[:], in0=flag_f[:], scalar1=0.0, scalar2=None,
                                    op0=ALU.is_gt).then_inc(s_flag, 1)
            dve.wait_ge(s_flag, 1)
            general = dve.value_load(flag[0:1, 0:1], min_val=0, max_val=1)

            with dve.If(general < 1):
                nc.vector.tensor_scalar(out=maxT[0:M2, :], in0=dscT[0:M2, :], scalar1=smax[:], scalar2=None,
                                        op0=ALU.add).then_inc(s_vset, 1)
            with dve.If(general > 0):
                nc.vector.tensor_copy(maxT[0:M2, :], sscT[0:M2, :]).then_inc(s_gv, 1)
                dve.wait_ge(s_gv, 1)
                dve.sem_clear(s_gv)
                with dve.Fori(0, T) as t:
                    with dve.Fori(0, TILE) as e:
                        u = dve.value_load(src_t[bass.ds(e, 1), bass.ds(t, 1)], min_val=0, max_val=N - 1)
                        v = dve.value_load(dst_t[bass.ds(e, 1), bass.ds(t, 1)], min_val=0, max_val=N)
                        nc.vector.tensor_tensor(out=maxT[0:M2, bass.ds(v, 1)], in0=maxT[0:M2, bass.ds(v, 1)],
                                                in1=sscT[0:M2, bass.ds(u, 1)], op=ALU.max).then_inc(s_gv, 1)
                        dve.wait_ge(s_gv, e + 1)
                        dve.nop(nofuse=True)
                    dve.sem_clear(s_gv)
                nc.vector.tensor_tensor(out=maxT[0:M2, :], in0=maxT[0:M2, :], in1=dscT[0:M2, :],
                                        op=ALU.add).then_inc(s_vset, 1)
            dve.wait_ge(s_vset, VS + 6)
            nc.vector.tensor_copy(winT[0:H, :], dscT[0:H, :])
            nc.vector.scalar_tensor_tensor(out=winT[32:M2, :], in0=maxT[32:M2, :], scalar=SLOPE, in1=maxT[32:M2, :],
                                           op0=ALU.mult, op1=ALU.max).then_inc(s_prep, 1)

            dve.wait_ge(s_prjc, NC)
            dve.wait_ge(s_self, 1)
            nc.vector.tensor_tensor(out=zself[:], in0=hw[:, :, D:ROW0], in1=hw[:, :, ROW0:HW],
                                    op=ALU.add).then_inc(s_sv, 1)
            dve.wait_ge(s_sv, 1)
            nc.vector.scalar_tensor_tensor(out=lself[:], in0=zself[:], scalar=SLOPE, in1=zself[:], op0=ALU.mult,
                                           op1=ALU.max).then_inc(s_sv, 1)
            dve.wait_ge(s_sv, 2)
            nc.vector.tensor_tensor(out=zself[:], in0=lself[:], in1=bank(7, NB * H).rearrange("p (b h) -> p b h", b=NB),
                                    op=ALU.subtract).then_inc(s_slog, 1)
            with dve.If(general > 0):
                dve.wait_ge(s_ghw, NC)
            dve.wait_ge(s_tab0, 16 * NC)
            dve.wait_ge(s_sp, 1)
            nc.vector.tensor_tensor(out=hw[:, :, 0:D].rearrange("p b (h c) -> p b h c", h=H),
                                    in0=hw[:, :, 0:D].rearrange("p b (h c) -> p b h c", h=H),
                                    in1=pself[:].unsqueeze(3).to_broadcast([P, NB, H, C]),
                                    op=ALU.mult).then_inc(s_sv, 1)
            xs3 = xs[:, :].rearrange("p (b f) -> p b f", b=NB)
            nc.vector.tensor_tensor(out=xs3, in0=xs3, in1=bias0_b[:].unsqueeze(1).to_broadcast([P, NB, D]),
                                    op=ALU.add).then_inc(s_sv, 1)

            def one_hot0(gi, s):
                nc.vector.tensor_tensor(
                    out=oh[:, s], in0=loc0[:, at(gi * G, G)].unsqueeze(2).to_broadcast([P, G, W0]),
                    in1=iota[:].unsqueeze(1).to_broadcast([P, G, W0]), op=ALU.is_equal).then_inc(s_oh, 1)

            def spread0(gi, s):
                dve.wait_ge(s_winp, gi + 1)
                nc.vector.tensor_tensor(
                    out=bdw[:], in0=bank(1, 4 * H, 64 * s).rearrange("p (k h) -> p k h", k=2).unsqueeze(2)
                    .to_broadcast([P, 2, 4, 2 * H]),
                    in1=quad[:].unsqueeze(1).unsqueeze(3).to_broadcast([P, 2, 4, 2 * H]),
                    op=ALU.mult).then_inc(s_bdw, 1)

            def add0(gi, s):
                n0 = [dve.value_load(first[0:1, at(gi * G + k * S0, 1)], min_val=0, max_val=N) for k in range(2)]
                dve.wait_ge(s_agg, gi + 1)
                for k in range(2):
                    dve.wait_ge(s_a0, gi * 4 + 2 * k + 1)
                    for table, part in ((aggT[:, bass.ds(n0[k], W0)], bank(3 + s, W0, k * W0)),
                                        (denT[0:H, bass.ds(n0[k], W0)], bank(5 + s, W0, k * W0)[0:H])):
                        nc.vector.tensor_tensor(out=table, in0=table, in1=part, op=ALU.add).then_inc(s_a0, 1)

            def attention(gi, s, nth):
                one_hot0(gi + 1, (s + 1) % SL)
                spread0(gi + 1, 1 - s % 2)
                dst = ade(s % 2).rearrange("p (t h) -> p t h", t=G)
                dve.wait_ge(got0[s], nth * (16 * G))
                dve.wait_ge(s_ade, gi + 1)
                nc.vector.tensor_tensor(out=zt[:], in0=g0[:, s, :, D:ROW0], in1=dst[:, :, 0:H],
                                        op=ALU.add).then_inc(s_v0, 1)
                dve.wait_ge(s_v0, gi * 3 + 1)
                nc.vector.scalar_tensor_tensor(out=lt[:], in0=zt[:], scalar=SLOPE, in1=zt[:], op0=ALU.mult,
                                               op1=ALU.max).then_inc(s_v0, 1)
                dve.wait_ge(s_v0, gi * 3 + 2)
                nc.vector.tensor_tensor(out=lt[:], in0=lt[:], in1=dst[:, :, H:2 * H],
                                        op=ALU.subtract).then_inc(s_v0, 1)
                dve.wait_ge(s_v0, gi * 3 + 3)
                nc.vector.tensor_scalar(out=zt[:], in0=lt[:], scalar1=0.0, scalar2=None,
                                        op0=ALU.min).then_inc(s_log, 1)
                dve.wait_ge(s_p, gi + 1)
                nc.vector.tensor_tensor(
                    out=msg[:, s % 2].rearrange("p t (h c) -> p t h c", h=H),
                    in0=g0[:, s, :, 0:D].rearrange("p t (h c) -> p t h c", h=H),
                    in1=pt[:, s % 2].unsqueeze(3).to_broadcast([P, G, H, C]), op=ALU.mult).then_inc(s_msg, 1)
                if not isinstance(gi, int):
                    add0(gi - 1, 1 - s % 2)

            with dve.If(general < 1):
                nc.vector.memset(mark[:, 5:6], 0.0).then_inc(s_a0, 1)
                one_hot0(0, 0)
                spread0(0, 0)
                groups(dve, attention)
                add0(NG - 1, 0)
                dve.wait_ge(s_a0, 4 * NG + 1)
            with dve.If(general > 0):
                dve.wait_ge(s_prep, 1)
                nc.vector.scalar_tensor_tensor(out=maxT[0:M2, :], in0=maxT[0:M2, :], scalar=SLOPE,
                                               in1=maxT[0:M2, :], op0=ALU.mult, op1=ALU.max).then_inc(s_gv, 1)
                dve.wait_ge(s_gv, 1)
                dve.sem_clear(s_gv)
                with dve.Fori(0, T) as t:
                    with dve.Fori(0, TILE) as e:
                        u = dve.value_load(src_t[bass.ds(e, 1), bass.ds(t, 1)], min_val=0, max_val=N - 1)
                        v = dve.value_load(dst_t[bass.ds(e, 1), bass.ds(t, 1)], min_val=0, max_val=N)
                        nc.vector.tensor_tensor(out=gz[:, bass.ds(e, 1)], in0=sscT[0:H, bass.ds(u, 1)],
                                                in1=dscT[0:H, bass.ds(v, 1)], op=ALU.add)
                        nc.vector.tensor_copy(gm[:, bass.ds(e, 1)], maxT[0:H, bass.ds(v, 1)]).then_inc(s_gv, 1)
                    dve.wait_ge(s_gv, TILE)
                    nc.vector.scalar_tensor_tensor(out=gz, in0=gz, scalar=SLOPE, in1=gz, op0=ALU.mult,
                                                   op1=ALU.max).then_inc(s_gv, 1)
                    dve.wait_ge(s_gv, TILE + 1)
                    nc.vector.tensor_tensor(out=gz, in0=gz, in1=gm, op=ALU.subtract).then_inc(s_gz, 1)
                    dve.wait_ge(s_gb, t + 1)
                    dve.nop(nofuse=True)
                    dve.sem_clear(s_gv)
                    with dve.Fori(0, TILE) as e:
                        u = dve.value_load(src_t[bass.ds(e, 1), bass.ds(t, 1)], min_val=0, max_val=N - 1)
                        v = dve.value_load(dst_t[bass.ds(e, 1), bass.ds(t, 1)], min_val=0, max_val=N)
                        nc.vector.tensor_tensor(out=denT[0:H, bass.ds(v, 1)], in0=denT[0:H, bass.ds(v, 1)],
                                                in1=gp[:, bass.ds(e, 1)], op=ALU.add)
                        nc.vector.scalar_tensor_tensor(
                            out=aggT[:, bass.ds(v, 1)], in0=hwT[:, bass.ds(u, 1)], scalar=ps[:, bass.ds(e, 1)],
                            in1=aggT[:, bass.ds(v, 1)], op0=ALU.mult, op1=ALU.add).then_inc(s_gv, 1)
                        dve.wait_ge(s_gv, e + 1)
                        dve.nop(nofuse=True)
                    dve.sem_clear(s_gv)
            nc.vector.memset(mark[:, 0:1], 0.0).then_inc(s_l0, 1)

            dve.wait_ge(s_sv, 4)

            def second(c, s):
                cb = at(c * CB, CB)
                xv = xs[:, at(c * CW, CW)].rearrange("p (b f) -> p b f", b=CB)
                den = bank(3, CB * H).rearrange("p (b h) -> p b h", b=CB)
                num = bank(4, CW).rearrange("p (b f) -> p b f", b=CB)
                t4 = tmp3.rearrange("p b (h c) -> p b h c", h=H)
                dve.wait_ge(s_mtp, c + 1)
                nc.vector.tensor_tensor(out=den_s[:], in0=pself[:, cb, :], in1=den, op=ALU.add).then_inc(s_vm, 1)
                nc.vector.tensor_tensor(out=tmp3, in0=hw[:, cb, 0:D], in1=num, op=ALU.add).then_inc(s_vm, 1)
                dve.wait_ge(s_vm, c * 5 + 1)
                nc.vector.reciprocal(rden[:], den_s[:]).then_inc(s_vm, 1)
                dve.wait_ge(s_vm, c * 5 + 3)
                nc.vector.tensor_tensor(out=t4, in0=t4, in1=rden[:].unsqueeze(3).to_broadcast([P, CB, H, C]),
                                        op=ALU.mult).then_inc(s_vm, 1)
                dve.wait_ge(s_vm, c * 5 + 4)
                nc.vector.tensor_tensor(out=xv, in0=xv, in1=tmp3, op=ALU.add).then_inc(s_vm, 1)
                dve.wait_ge(s_vm, c * 5 + 5)
                dve.nop(nofuse=True)
                statistics(c + NC, c)
                scales(c + NC)

            pairs(dve, second)
            dve.wait_ge(s_hl, NC)
            nc.vector.memset(big[:], 0.0).then_inc(s_zero, 1)
            dve.wait_ge(s_zero, 1)

            def select1(gi, s):
                nc.vector.tensor_tensor(
                    out=oh[:, 0], in0=typ_f[:, at(gi * G, G)].unsqueeze(2).to_broadcast([P, G, R]),
                    in1=iota[:].unsqueeze(1).to_broadcast([P, G, R]), op=ALU.is_equal).then_inc(s_oe, 1)
                if not (isinstance(gi, int) and gi == 0):
                    dve.wait_ge(s_sel, gi)
                nc.vector.tensor_tensor(
                    out=oh1[:], in0=loc1[:, at(gi * G, G)].unsqueeze(2).to_broadcast([P, G, W1]),
                    in1=iota[:, 0:W1].unsqueeze(1).to_broadcast([P, G, W1]), op=ALU.is_equal).then_inc(s_v1, 1)
                dve.wait_ge(s_cop, gi + 1)
                nc.vector.tensor_tensor(
                    out=coef[:], in0=bank(1, G * B).rearrange("p (t b) -> p t b", t=G),
                    in1=wgt[:, at(gi * G, G)].unsqueeze(2).to_broadcast([P, G, B]), op=ALU.mult).then_inc(s_v1, 1)
                dve.wait_ge(s_v1, gi * 2 + 2)
                nc.vector.tensor_tensor(
                    out=sel1[:, s], in0=oh1[:].unsqueeze(2).to_broadcast([P, G, B, W1]),
                    in1=coef[:].unsqueeze(3).to_broadcast([P, G, B, W1]), op=ALU.mult).then_inc(s_sel, 1)

            def relational(gi, s, nth):
                select1(gi + 1, 1 - s % 2)
                n0 = [dve.value_load(first[0:1, at(gi * G + k * S1, 1)], min_val=0, max_val=N)
                      for k in range(G // S1)]
                dve.wait_ge(s_agg1, gi + 1)
                for k in range(G // S1):
                    if k or not isinstance(gi, int):
                        dve.wait_ge(s_a1, gi * 4 + k)
                    table = agg1[:, :, bass.ds(n0[k], W1)]
                    nc.vector.tensor_tensor(
                        out=table, in0=table,
                        in1=bank(2 + s % 2, B * W1, k * B * W1).rearrange("p (b w) -> p b w", b=B),
                        op=ALU.add).then_inc(s_a1, 1)

            with dve.If(general < 1):
                select1(0, 0)
                groups(dve, relational)
                dve.wait_ge(s_a1, 4 * NG)
            with dve.If(general > 0):
                with dve.Fori(0, T) as t:
                    nc.vector.tensor_tensor(out=oh[:, 0, 0, :], in0=typ_f[:, bass.ds(t, 1)].to_broadcast([P, R]),
                                            in1=iota[:], op=ALU.is_equal).then_inc(s_oe, 1)
                    dve.wait_ge(s_oep, t + 1)
                    nc.vector.tensor_copy(ohT[0:R, 0, :], bank(0, P)[0:R]).then_inc(s_oeT, 1)
                    dve.wait_ge(s_cop, t + 1)
                    nc.vector.tensor_tensor(out=coef[:, 0, :], in0=bank(1, B),
                                            in1=wgt[:, bass.ds(t, 1)].to_broadcast([P, B]),
                                            op=ALU.mult).then_inc(s_gc, 1)
                    dve.wait_ge(s_gr, t * 16 + 16)
                    dve.nop(nofuse=True)
                    with dve.Fori(0, TILE) as e:
                        u = dve.value_load(src_t[bass.ds(e, 1), bass.ds(t, 1)], min_val=0, max_val=N - 1)
                        v = dve.value_load(dst_t[bass.ds(e, 1), bass.ds(t, 1)], min_val=0, max_val=N)
                        nc.vector.scalar_tensor_tensor(
                            out=agg1[:, :, bass.ds(v, 1)].rearrange("p b o -> p (b o)"), in0=gcb[:, bass.ds(e * B, B)],
                            scalar=h1T[:, bass.ds(u, 1)],
                            in1=agg1[:, :, bass.ds(v, 1)].rearrange("p b o -> p (b o)"), op0=ALU.mult,
                            op1=ALU.add).then_inc(s_gv, 1)
                        dve.wait_ge(s_gv, e + 1)
                        dve.nop(nofuse=True)
                    dve.sem_clear(s_gv)
            nc.vector.memset(mark[:, 2:3], 0.0).then_inc(s_l1, 1)


            for k in range(2):
                nc.vector.memset(mark[:, 3 + k:4 + k], 0.0).then_inc(s_fo, 1)

            def finish(n, s, stores):
                dve.wait_ge(s_fp, n + 3)
                if stores is not None:
                    dve.wait_ge(s_out[s], stores)
                blk = at(n * P, P)
                nc.vector.tensor_tensor(out=pre[:, s, :], in0=hl[:, blk], in1=bank(3 + s, D),
                                        op=ALU.add).then_inc(s_fv, 1)
                dve.wait_ge(s_fv, n + 1)
                nc.vector.scalar_tensor_tensor(out=outc[:, s, :], in0=pre[:, s, :], scalar=0.0, in1=xs[:, blk],
                                               op0=ALU.max, op1=ALU.add).then_inc(s_fo, 1)

            finish(0, 0, None)
            finish(1, 1, None)
            with dve.Fori(1, NB // 2) as i:
                finish(i * 2, 0, i * 16)
                finish(i * 2 + 1, 1, i * 16)
            finish(NB - 1, 0, NB // 2 * 16)

        @block.tensor
        def _(pe):
            mm, tr = nc.tensor.matmul, nc.tensor.transpose

            def cols(at, n, rows=P):
                return ps[0:rows, at:at + n]

            def blocks(src, col):
                for k in range(CB):
                    last = tr(cols(col + k * P, P), src[:, k * P:k * P + P], ident[:])
                return last

            pe.wait_ge(s_const, 16 * CONST_DMAS)
            pe.wait_ge(s_gset, 3)
            tr(cols(0, P), w_sb[:], ident[:]).then_inc(s_pset, 1)
            pe.wait_ge(s_vset, 9)
            mm(cols(512, 2 * H), wT[:], att_m[:], start=True, stop=True).then_inc(s_pset, 1)
            pe.wait_ge(s_vset, VS)
            def prepare(c, s):
                pe.wait_ge(s_hc, c + 1)
                blocks(hc[:, s], 0).then_inc(s_hcp, 1)
                pe.wait_ge(s_hcT, c + 1)
                for k in range(CB):
                    last = mm(cols(1024 + k * 256, HW), hcT[:, k * P:k * P + P], wcat[:], start=True, stop=True)
                last.then_inc(s_prj, 1)
                pe.wait_ge(s_scc, c + 1)
                for lo, hi in ((0, 512), (512, CW)):
                    last = mm(cols(5 * 512 + lo, hi - lo, 64 + M2), w_sc[:], hcT[:, lo:hi], start=True, stop=True)
                last.then_inc(s_sc, 1)

            pairs(pe, prepare)
            pe.wait_ge(s_vset, VS + 4)
            mm(cols(7 * 512, 2, 1), ones[:, 0:1], bad[:, 0:2], start=True, stop=True).then_inc(s_pset, 1)
            pe.wait_ge(s_flag, 1)
            general = pe.value_load(flag[0:1, 0:1], min_val=0, max_val=1)

            with pe.If(general > 0):
                with pe.Fori(0, NC) as c:
                    pe.wait_ge(s_gst, c + 1)
                    blocks(stg, 0).then_inc(s_gt, 1)
            pe.wait_ge(s_prep, 1)
            for b in range(NB):
                last = tr(cols(7 * 512 + b * H, H), winT[32:M2, b * P:b * P + P], ident[32:M2, 32:M2])
            last.then_inc(s_self, 1)

            def turn(gi, s, ready, done):
                pe.wait_ge(ready, gi + 1)
                for k in range(2):
                    last = tr(cols(k * P, P), oh[:, s, k * 4:k * 4 + 4, :].rearrange("p t w -> p (t w)"), ident[:])
                last.then_inc(done, 1)

            def window0(gi, s):
                pe.wait_ge(s_awin, gi + 1)
                for k in range(2):
                    last = mm(cols(512 + 64 * s + k * 2 * H, 2 * H), awin[:, k].rearrange("p q w -> p (q w)"), pick[:],
                              start=True, stop=True)
                last.then_inc(s_winp, 1)

            def scores0(gi, s):
                pe.wait_ge(s_ohT, gi + 1)
                pe.wait_ge(s_bdw, gi + 1)
                for k in range(2):
                    last = mm(ade(s)[:, k * 8 * H:k * 8 * H + 8 * H], ohT[:, k, :], bdw[:, k].rearrange("p q h -> p (q h)"),
                              start=True, stop=True)
                last.then_inc(s_ade, 1)

            def attention(gi, s, nth):
                turn(gi + 1, (s + 1) % SL, s_oh, s_ohp)
                scores0(gi + 1, 1 - s % 2)
                window0(gi + 2, s % 2)
                pe.wait_ge(s_msg, gi + 1)
                for k in range(2):
                    for j in range(S0):
                        t = k * S0 + j
                        mm(cols((3 + s % 2) * 512 + k * W0, W0), msg[:, s % 2, t, :], oh[:, s, t, :], start=(j == 0),
                           stop=(j == S0 - 1))
                    for j in range(S0):
                        t = k * S0 + j
                        last = mm(cols((5 + s % 2) * 512 + k * W0, W0, H), pt[:, s % 2, t, :], oh[:, s, t, :],
                                  start=(j == 0), stop=(j == S0 - 1))
                last.then_inc(s_agg, 1)

            with pe.If(general < 1):
                turn(0, 0, s_oh, s_ohp)
                window0(0, 0)
                scores0(0, 0)
                window0(1, 1)
                groups(pe, attention)
            with pe.If(general > 0):
                with pe.Fori(0, T) as t:
                    pe.wait_ge(s_gp, t + 1)
                    mm(cols(0, TILE), head_to[:], gp, start=True, stop=True).then_inc(s_gb, 1)

            def sums(c):
                pe.wait_ge(s_mst, c * 2 + 2)
                blocks(stg, 4 * 512)
                for k in range(CB):
                    last = tr(cols(3 * 512 + k * H, H), dstg[:, k * P:k * P + P], ident[0:H, 0:H])
                last.then_inc(s_mtp, 1)

            def second(c, s):
                if not last_chunk(c):
                    pe.wait_ge(s_vm, c * 5 + 4)
                    sums(c + 1)
                pe.wait_ge(s_hc, c + NC + 1)
                blocks(hc[:, s], 0).then_inc(s_h1p, 1)
                pe.wait_ge(s_h1T, c * 2 + 1)
                for k in range(CB):
                    mm(cols(6 * 512 + k * P, P), hcT[:, k * P:k * P + P], loop_sb[:], start=True, stop=False)
                    last = mm(cols(6 * 512 + k * P, P), ones[0:1, :], bias1_b[0:1, :], start=False, stop=True)
                last.then_inc(s_hlp, 1)

            sums(0)
            pairs(pe, second)
            pe.wait_ge(s_h1T, 2 * NC)

            def coefs1(gi):
                turn(gi, 0, s_oe, s_oep)
                pe.wait_ge(s_oeT, gi + 1)
                for k in range(2):
                    last = mm(cols(512 + k * 4 * B, 4 * B), ohT[:, k, :], comp_bd[:].rearrange("p q b -> p (q b)"),
                              start=True, stop=True)
                last.then_inc(s_cop, 1)

            def relational(gi, s, nth):
                coefs1(gi + 1)
                pe.wait_ge(s_sel, gi + 1)
                pe.wait_ge(got1[s], nth * (16 * G))
                for t in range(G):
                    last = mm(cols((2 + s % 2) * 512 + t // S1 * B * W1, B * W1), g1[:, s, t, :],
                              sel1[:, s % 2, t].rearrange("p b w -> p (b w)"), start=(t % S1 == 0),
                              stop=(t % S1 == S1 - 1))
                last.then_inc(s_agg1, 1)

            with pe.If(general < 1):
                coefs1(0)
                groups(pe, relational)
            with pe.If(general > 0):
                with pe.Fori(0, T) as t:
                    pe.wait_ge(s_oe, t + 1)
                    tr(cols(0, P, R), oh[:, 0, 0, :], ident[:]).then_inc(s_oep, 1)
                    pe.wait_ge(s_oeT, t + 1)
                    mm(cols(512, B), ohT[0:R, 0, :], comp4[0:R, :], start=True, stop=True).then_inc(s_cop, 1)

            for _ in range(2):
                pe.sem_inc(s_fp, 1)

            def product(n, s):
                pe.wait_ge(s_fst, n + 1)
                pe.wait_ge(s_fo, n + 1)
                for b in range(B):
                    last = mm(cols((3 + s) * 512, D), aggc[:, s, b, :], basis_sb[:, b, :], start=(b == 0),
                              stop=(b == B - 1))
                last.then_inc(s_fp, 1)

            with pe.Fori(0, NB // 2) as i:
                product(i * 2, 0)
                product(i * 2 + 1, 1)
            product(NB - 1, 0)


def kernel(x, src, dst, edge_type_32, edge_weight1, L0_gnn_W, L0_gnn_att_src, L0_gnn_att_dst, L0_gnn_bias,
           L1_gnn_weight, L1_gnn_w_comp, L1_gnn_loop_weight, L1_gnn_h_bias):
    import numpy as np
    import concourse.bacc as bacc
    from concourse.bass_utils import run_bass_kernel_spmd

    def tiles(a, pad, n):
        full = np.full(n * TILE, pad, a.dtype)
        full[:E] = a.reshape(-1)
        return np.ascontiguousarray(full.reshape(n, TILE).T)

    xp = np.zeros((NP, D), x.dtype)
    xp[:N] = x
    arrays = {
        "x_pad": xp, "src_t": tiles(src, 0, TT), "dst_t": tiles(dst, N, TT),
        "typ_t": tiles(edge_type_32, 0, TT), "wgt_t": tiles(edge_weight1, 0, TT), "w_att": L0_gnn_W,
        "att_src": L0_gnn_att_src, "att_dst": L0_gnn_att_dst, "bias0": L0_gnn_bias, "basis": L1_gnn_weight,
        "w_comp": L1_gnn_w_comp, "w_loop": L1_gnn_loop_weight, "bias1": L1_gnn_h_bias,
    }
    nc = bacc.Bacc("TRN2", target_bir_lowering=False, num_devices=1)
    arrays = {k: np.ascontiguousarray(v) for k, v in arrays.items()}
    args = [nc.dram_tensor(k, v.shape, mybir.dt.from_np(v.dtype), kind="ExternalInput").ap()
            for k, v in arrays.items()]
    out = nc.dram_tensor("out", (NP, D), mybir.dt.float32, kind="ExternalOutput").ap()
    build(nc, *args, out)
    res = run_bass_kernel_spmd(nc, [arrays], core_ids=[0])
    return res.results[0]["out"][:N]
```

```python
from contextlib import ExitStack

import concourse.bass as bass
from concourse import mybir

P = 128
N, E, D, H, C, R, B = 3125, 103125, 128, 8, 16, 32, 8
TILE = 128
G = 8
SL = 4
NG = -(-(E - TILE * G) // (TILE * G * SL)) * SL + 1
T = NG * G
TT = T + SL * G
NI = (NG - 1) // SL
G_LAST = -(-E // TILE) - (NG - 1) * G
W0, S0 = 32, 4
W1, S1 = 16, 2
NB = -(-N // P)
NP = NB * P
CB = 5
NC = NB // CB
CW = CB * P
ROW0 = D + H
HW = D + 2 * H
SPREAD = 60.0
EPS = 1e-5
SLOPE = 0.2
LAG = 2
IN_LOOP = NI - LAG
LATE = (NB - 2, NB - 1)
assert IN_LOOP == LATE[0]
READY = (LAG * SL + 2) * G
VS = 15
M2 = 32 + H


def build(nc, x, src_t, dst_t, typ_t, wgt_t, w_att, att_src, att_dst, bias0, basis,
          w_comp, w_loop, bias1, out):
    f32, i32 = mybir.dt.float32, mybir.dt.int32
    ALU, ACT, AX = mybir.AluOpType, mybir.ActivationFunctionType, mybir.AxisListType
    ctx = ExitStack()
    with ctx:
        def sb(name, shape, dt=f32):
            return ctx.enter_context(nc.sbuf_tensor(name, shape, dt))

        def sem(name):
            return ctx.enter_context(nc.semaphore(name))

        table0 = nc.dram_tensor("table0", (NP, ROW0), f32, kind="Internal").ap()
        table1 = nc.dram_tensor("table1", (NP, D), f32, kind="Internal").ap()
        coef_row = nc.dram_tensor("coef_row", (TILE, B), f32, kind="Internal").ap()

        src_i = sb("src_i", [P, TT], i32)
        loc = sb("loc", [P, 2, TT])
        loc0, loc1 = loc[:, 0, :], loc[:, 1, :]
        typ_f = sb("typ_f", [P, TT])
        wgt = sb("wgt", [P, TT])
        xs = sb("xs", [P, NB * D])
        h1T = sb("h1T", [P, NP])
        hl = sb("hl", [P, NP])
        big = sb("big", [P, B * NP])
        agg1 = big[:, :].rearrange("p (b n) -> p b n", b=B)
        aggT = big[:, 0:NP]
        denT = big[:, NP:2 * NP]
        winT = big[:, 2 * NP:3 * NP]
        dscT = big[:, 3 * NP:4 * NP]
        sscT = big[:, 4 * NP:5 * NP]
        maxT = big[:, 5 * NP:6 * NP]
        hw = big[:, 6 * NP:6 * NP + NB * HW].rearrange("p (b f) -> p b f", b=NB)

        ones = sb("ones", [P, P])
        ident = sb("ident", [P, P])
        iota_i = sb("iota_i", [P, W0], i32)
        iota = sb("iota", [P, W0])
        quad = sb("quad", [P, 4])
        head_of = sb("head_of", [P, H])
        head_to = sb("head_to", [H, P])
        pick = sb("pick", [M2, 2 * H])
        w_sb = sb("w_sb", [P, D])
        wT = sb("wT", [P, D])
        att_c = sb("att_c", [P, 2])
        att_m = sb("att_m", [P, 2 * H])
        wcat = sb("wcat", [P, HW])
        w_sc = sb("w_sc", [P, 64 + M2])
        comp4 = sb("comp4", [P, B])
        comp_bd = sb("comp_bd", [P, 4, B])
        basis_sb = sb("basis_sb", [P, B, D])
        loop_sb = sb("loop_sb", [P, D])
        bias0_b = sb("bias0_b", [P, D])
        bias1_b = sb("bias1_b", [P, D])
        eps_t = sb("eps_t", [P, 1])
        smax = sb("smax", [M2, 1])
        smin = sb("smin", [M2, 1])
        high = sb("high", [P, 2, 2])
        low = sb("low", [P, 2, 2])
        least = sb("least", [1, 1])
        bad = sb("bad", [P, 10])
        mark = sb("mark", [P, 7])
        flag_f = sb("flag_f", [1, 1])
        flag = sb("flag", [1, 1], i32)
        den_s = sb("den_s", [P, H])
        rden = sb("rden", [P, H])
        stats = sb("stats", [P, CB, 6])
        mv = sb("mv", [P, NB, 2])
        nmr = sb("nmr", [P, NB])
        smc = sb("smc", [M2, 2, NC])
        rinv = sb("rinv", [P, NB])
        rstd = sb("rstd", [P, NB])

        work = sb("work", [P, SL * G * ROW0 + 3 * G * D])
        GW = SL * G * ROW0
        g0 = work[:, 0:GW].rearrange("p (s t f) -> p s t f", s=SL, t=G)
        msg = work[:, GW:GW + 2 * G * D].rearrange("p (s t f) -> p s t f", s=2, t=G)
        g1 = work[:, 0:SL * G * D].rearrange("p (s t f) -> p s t f", s=SL, t=G)
        sel1 = work[:, GW:GW + 2 * G * D].rearrange("p (s t b w) -> p s t b w", s=2, t=G, b=B)
        hc = work[:, 0:2 * CW].rearrange("p (s f) -> p s f", s=2)
        hcT = work[:, 2 * CW:3 * CW]
        stg = work[:, 4 * CW:5 * CW]
        num_b, den_b, row_b, h1_b, h1T_b = (work[:, GW + 2 * G * D + k * P:GW + 2 * G * D + (k + 1) * P]
                                            for k in range(5))
        basei = big[:, 5 * NP:5 * NP + TT].bitcast(i32)
        dst_i = big[:, 5 * NP + TT:5 * NP + 2 * TT].bitcast(i32)
        typ_i = big[:, 5 * NP + 2 * TT:5 * NP + 3 * TT].bitcast(i32)
        behind = hl[0:1, 0:IN_LOOP * SL * G].bitcast(i32)
        ahead = hl[0:1, IN_LOOP * SL * G:2 * IN_LOOP * SL * G]
        gz, gm, gp = (work[0:H, k * TILE:k * TILE + TILE] for k in range(3))
        hwT = work[:, GW + 3 * G * D - NP:GW + 3 * G * D]
        gcb = work[:, GW:GW + TILE * B]
        aggc = work[:, GW + 2 * G * D:GW + 2 * G * D + B * P].rearrange("p (b n) -> p b n", b=B)
        aggc_late = work[:, GW:GW + B * P].rearrange("p (b n) -> p b n", b=B)
        pre = work[:, SL * G * D:SL * G * D + P]
        outc = work[:, SL * G * D + P:SL * G * D + 2 * P]

        first = sb("first", [1, TT], i32)
        idx = sb("idx", [P, SL, G], i32)
        oh = sb("oh", [P, SL, G, W0])
        ohT = sb("ohT", [P, 2, P])
        awin = sb("awin", [M2, 2, 4, W0])
        bdw = sb("bdw", [P, 2, 4, 2 * H])
        zt = sb("zt", [P, G, H])
        lt = sb("lt", [P, G, H])
        pt = sb("pt", [P, 2, G, H])
        oh1 = sb("oh1", [P, G, W1])
        coef = sb("coef", [P, G, B])
        pself = sb("pself", [P, NB, H])
        zself = sb("zself", [P, NB, H])
        lself = sb("lself", [P, NB, H])

        ps = ctx.enter_context(nc.psum_tensor("ps", [P, 8 * 512], f32))

        def at(start, size):
            return slice(start, start + size) if isinstance(start, int) else bass.ds(start, size)

        def bank(k, cols, off=0):
            return ps[:, k * 512 + off:k * 512 + off + cols]

        s_const = sem("s_const")
        s_att = sem("s_att")
        s_edges = sem("s_edges")
        s_x = sem("s_x")
        s_xr = sem("s_xr")
        s_src = sem("s_src")
        s_gset = sem("s_gset")
        s_vset = sem("s_vset")
        s_pset = sem("s_pset")
        s_loc = sem("s_loc")
        s_flag = sem("s_flag")
        s_hc = sem("s_hc")
        s_sqrt = sem("s_sqrt")
        s_var = sem("s_var")
        s_hcp = sem("s_hcp")
        s_hcT = sem("s_hcT")
        s_prj = sem("s_prj")
        s_prjc = sem("s_prjc")
        s_sc = sem("s_sc")
        s_scc = sem("s_scc")
        s_smc = sem("s_smc")
        s_tab0 = sem("s_tab0")
        s_prep = sem("s_prep")
        got0 = [sem(f"got0_{s}") for s in range(SL)]
        got1 = [sem(f"got1_{s}") for s in range(SL)]
        s_idx = sem("s_idx")
        s_oh = sem("s_oh")
        s_ohp = sem("s_ohp")
        s_ohT = sem("s_ohT")
        s_awin = sem("s_awin")
        s_winp = sem("s_winp")
        s_bdw = sem("s_bdw")
        s_ade = sem("s_ade")
        s_log = sem("s_log")
        s_p = sem("s_p")
        s_msg = sem("s_msg")
        s_agg = sem("s_agg")
        s_v0 = sem("s_v0")
        s_a0 = sem("s_a0")
        s_l0 = sem("s_l0")
        s_win = sem("s_win")
        s_idx1 = sem("s_idx1")
        s_oe = sem("s_oe")
        s_oep = sem("s_oep")
        s_oeT = sem("s_oeT")
        s_cop = sem("s_cop")
        s_sel = sem("s_sel")
        s_agg1 = sem("s_agg1")
        s_a1 = sem("s_a1")
        s_v1 = sem("s_v1")
        s_nmr = sem("s_nmr")
        s_self = sem("s_self")
        s_slog = sem("s_slog")
        s_sp = sem("s_sp")
        s_v2 = sem("s_v2")
        s_sv = sem("s_sv")
        s_mst = sem("s_mst")
        s_mtp = sem("s_mtp")
        s_vm = sem("s_vm")
        s_bn = sem("s_bn")
        s_inv = sem("s_inv")
        s_h1p = sem("s_h1p")
        s_h1T = sem("s_h1T")
        s_hlp = sem("s_hlp")
        s_hl = sem("s_hl")
        s_hfree = sem("s_hfree")
        s_tab1 = sem("s_tab1")
        s_zero = sem("s_zero")
        s_zrest = sem("s_zrest")
        s_fst = sem("s_fst")
        s_fp = sem("s_fp")
        s_fv = sem("s_fv")
        s_fo = sem("s_fo")
        s_out = sem("s_out")
        s_ofree = sem("s_ofree")
        s_gv = sem("s_gv")
        s_gst = sem("s_gst")
        s_gt = sem("s_gt")
        s_ghw = sem("s_ghw")
        s_gz = sem("s_gz")
        s_gp = sem("s_gp")
        s_gb = sem("s_gb")
        s_gc = sem("s_gc")
        s_gw = sem("s_gw")
        s_gr = sem("s_gr")

        block = ctx.enter_context(nc.Block())

        def ade(par):
            return bank(7 if par else 2, 2 * 4 * 2 * H)

        def pairs(eng, step):
            with eng.Fori(0, NC // 2) as i:
                step(i * 2, 0)
                step(i * 2 + 1, 1)
            step(NC - 1, 0)

        def last_chunk(c):
            return isinstance(c, int) and c == NC - 1

        def groups(eng, step, block_part=None):
            step(0, 0, 1)

            def turn(i, parts):
                for k in range(1, SL + 1):
                    step(i * SL + k, k % SL, i + 1 + k // SL)
                    if parts is not None:
                        parts(k, i - LAG)

            if block_part is not None:
                with eng.Fori(0, LAG) as i:
                    turn(i, None)
            with eng.Fori(LAG if block_part else 0, NI - 1) as i:
                turn(i, block_part)
            turn(NI - 1, block_part)

        def exists(gi):
            return not isinstance(gi, int) or gi < NG

        def is_first(gi):
            return isinstance(gi, int) and gi == 0

        def gathered(gi, nth):
            return nth * (16 * G) if exists(gi + 1) else nth * (16 * G) - 16 * (G - G_LAST)

        CONST_DMAS = 8
        EDGE_DMAS = 5

        @block.sync
        def _(sp):
            for lo, hi, arrived in ((0, CB, s_x), (CB, NB, s_xr)):
                sp.dma_start(xs[:, lo * D:hi * D].rearrange("p (b f) -> p b f", b=hi - lo),
                             x[lo * P:hi * P, :].rearrange("(b p) f -> p b f", p=P)).then_inc(arrived, 16)
            sp.dma_start(src_i[:], src_t).then_inc(s_src, 16)
            sp.dma_start(dst_i, dst_t).then_inc(s_edges, 16)
            sp.dma_start(basei, dst_t[0, :].partition_broadcast(P)).then_inc(s_edges, 16)
            sp.dma_start(first[:], dst_t[0:1, :]).then_inc(s_edges, 16)
            sp.dma_start(typ_i, typ_t).then_inc(s_edges, 16)
            sp.dma_start(wgt[:], wgt_t).then_inc(s_edges, 16)
            for q in range(4):
                sp.dma_start(comp4[32 * q:32 * q + R, :], w_comp).then_inc(s_const, 16)
            sp.dma_start(basis_sb[:], basis.rearrange("b d f -> d b f")).then_inc(s_const, 16)
            sp.dma_start(loop_sb[:], w_loop).then_inc(s_const, 16)
            sp.dma_start(bias0_b[:], bias0.partition_broadcast(P)).then_inc(s_const, 16)
            sp.dma_start(bias1_b[:], bias1.partition_broadcast(P)).then_inc(s_const, 16)
            with sp.Fori(0, NC) as c:
                sp.wait_ge(s_prjc, c + 1)
                sp.dma_start(table0[bass.ds(c * CW, CW), :].rearrange("(b p) f -> p b f", p=P),
                             hw[:, bass.ds(c * CB, CB), 0:ROW0]).then_inc(s_tab0, 16)
            sp.sem_inc(s_hfree, 1)
            with sp.Fori(0, NB) as n:
                sp.wait_ge(s_hc, n + NC + 1)
                sp.dma_start(table1[bass.ds(n * P, P), :], h1_b).then_inc(s_tab1, 16)
                sp.wait_ge(s_tab1, n * 16 + 16)
                sp.sem_inc(s_hfree, 1)

            sp.wait_ge(s_flag, 1)
            general = sp.value_load(flag[0:1, 0:1], min_val=0, max_val=1)
            with sp.If(general > 0):
                with sp.Fori(0, T) as t:
                    sp.wait_ge(s_gc, t + 1)
                    sp.dma_start(coef_row, coef[:, 0, :]).then_inc(s_gw, 16)
                    sp.wait_ge(s_gw, t * 16 + 16)
                    sp.dma_start(gcb,
                                 coef_row.rearrange("(o e) b -> o (e b)", o=1)[0].partition_broadcast(P)
                                 ).then_inc(s_gr, 16)

            def store(n):
                sp.wait_ge(s_fo, n + 1)
                sp.dma_start(out[at(n * P, P), :], outc).then_inc(s_out, 16)
                sp.wait_ge(s_out, n * 16 + 16)
                sp.sem_inc(s_ofree, 1)

            sp.sem_inc(s_ofree, 1)
            with sp.Fori(0, NB) as n:
                store(n)

        @block.gpsimd
        def _(pool):
            nc.gpsimd.iota(iota_i[:], pattern=[[1, W0]], base=0, channel_multiplier=0).then_inc(s_gset, 1)
            nc.gpsimd.memset(ones[:], 1.0).then_inc(s_gset, 1)
            pool.wait_ge(s_gset, 2)
            nc.gpsimd.affine_select(out=ident[:], in_=ones[:], pattern=[[-1, P]], base=0, channel_multiplier=1,
                                    compare_op=ALU.is_equal, fill=0.0).then_inc(s_gset, 1)
            nc.gpsimd.affine_select(out=head_of[:], in_=ones[:, 0:H], pattern=[[-C, H]], base=0,
                                    channel_multiplier=1, compare_op=ALU.is_ge, fill=0.0).then_inc(s_gset, 1)
            nc.gpsimd.affine_select(out=quad[:], in_=ones[:, 0:4], pattern=[[-32, 4]], base=0,
                                    channel_multiplier=1, compare_op=ALU.is_ge, fill=0.0).then_inc(s_gset, 1)
            nc.gpsimd.affine_select(out=head_to[:], in_=ones[0:H, :], pattern=[[1, P]], base=0,
                                    channel_multiplier=-C, compare_op=ALU.is_ge, fill=0.0).then_inc(s_gset, 1)
            nc.gpsimd.affine_select(out=pick[:, 0:H], in_=ones[0:M2, 0:H], pattern=[[-1, H]], base=0,
                                    channel_multiplier=1, compare_op=ALU.is_equal, fill=0.0).then_inc(s_gset, 1)
            nc.gpsimd.affine_select(out=pick[:, H:2 * H], in_=ones[0:M2, 0:H], pattern=[[-1, H]], base=-32,
                                    channel_multiplier=1, compare_op=ALU.is_equal, fill=0.0).then_inc(s_gset, 1)
            pool.wait_ge(s_gset, 8)
            nc.gpsimd.affine_select(out=head_of[:], in_=head_of[:], pattern=[[C, H]], base=C - 1,
                                    channel_multiplier=-1, compare_op=ALU.is_ge, fill=0.0).then_inc(s_gset, 1)
            nc.gpsimd.affine_select(out=quad[:], in_=quad[:], pattern=[[32, 4]], base=31,
                                    channel_multiplier=-1, compare_op=ALU.is_ge, fill=0.0).then_inc(s_gset, 1)
            nc.gpsimd.affine_select(out=head_to[:], in_=head_to[:], pattern=[[-1, P]], base=C - 1,
                                    channel_multiplier=C, compare_op=ALU.is_ge, fill=0.0).then_inc(s_gset, 1)
            nc.gpsimd.iota(behind, pattern=[[P, IN_LOOP], [0, SL * G]], base=P,
                           channel_multiplier=0).then_inc(s_gset, 1)
            nc.gpsimd.memset(aggT, 0.0).then_inc(s_gset, 1)
            nc.gpsimd.memset(denT[0:H], 0.0).then_inc(s_gset, 1)
            pool.wait_ge(s_edges, 16 * EDGE_DMAS)
            nc.gpsimd.tensor_copy(typ_f[:], typ_i).then_inc(s_gset, 1)

            pool.wait_ge(s_flag, 1)
            general = pool.value_load(flag[0:1, 0:1], min_val=0, max_val=1)

            def gathers(table, g, got, staged):
                def step(gi, s, nth):
                    pool.wait_ge(staged, gi + 1)
                    pool.nop(nofuse=True)
                    for t in range(G if exists(gi + 1) else G_LAST):
                        nc.gpsimd.indirect_dma_start(
                            out=g[:, s, t, :], out_offset=None, in_=table,
                            in_offset=bass.IndirectOffsetOnAxis(ap=idx[:, s, t:t + 1], axis=0),
                        ).then_inc(got[s], 16)
                groups(pool, step)

            pool.wait_ge(s_tab0, 16 * NC)
            with pool.If(general < 1):
                gathers(table0, g0, got0, s_idx)
            pool.wait_ge(s_l0, 1)
            pool.wait_ge(s_win, 1)
            nc.gpsimd.memset(big[:, 2 * NP:4 * NP], 0.0).then_inc(s_zrest, 1)
            pool.wait_ge(s_tab1, 16 * NB)
            with pool.If(general < 1):
                gathers(table1, g1, got1, s_idx1)

        @block.scalar
        def _(act):
            def root(variances, blk):
                act.wait_ge(s_var, variances)
                nc.scalar.activation(rstd[:, blk], mv[:, blk, 1], ACT.Sqrt, bias=eps_t[:],
                                     scale=1.0).then_inc(s_sqrt, 1)

            def normalise(nth, c, s, col):
                act.wait_ge(s_nmr, nth + 1)
                for k in range(CB):
                    last = nc.scalar.activation(hc[:, s, k * D:k * D + D], xs[:, at(c * CW + k * D, D)], ACT.Relu,
                                                bias=nmr[:, at(col + k, 1)], scale=rinv[:, at(col + k, 1)])
                last.then_inc(s_hc, 1)

            def features(c):
                act.wait_ge(s_hcp, c + 1)
                nc.scalar.copy(hcT, bank(0, CW)).then_inc(s_hcT, 1)

            def prepare(c, s):
                if not last_chunk(c):
                    normalise(1, c + 1, 1 - s, (c + 1) * CB)
                act.wait_ge(s_prj, c + 1)
                nc.scalar.copy(hw[:, at(c * CB, CB), :],
                               ps[:, 1024:1024 + CB * 256].rearrange("p (b f) -> p b f", b=CB)[:, :, 0:HW]
                               ).then_inc(s_prjc, 1)
                if not last_chunk(c):
                    features(c + 1)

            def load_root():
                return nc.scalar.activation(mark[:, 6:7], eps_t[:], ACT.Sqrt)

            act.dma_start(w_sb[:], w_att).then_inc(s_att, 16)
            act.dma_start(att_c[:, 0:1], att_src.rearrange("h (c o) -> (h c) o", o=1)).then_inc(s_att, 16)
            act.dma_start(att_c[:, 1:2], att_dst.rearrange("h (c o) -> (h c) o", o=1)).then_inc(s_att, 16)
            act.wait_ge(s_vset, 1)
            load_root()
            root(1, slice(0, CB))
            normalise(0, 0, 0, 0)
            features(0)
            root(NC, slice(CB, NB))
            pairs(act, prepare)
            act.wait_ge(s_src, 16)
            act.wait_ge(s_flag, 1)
            general = act.value_load(flag[0:1, 0:1], min_val=0, max_val=1)

            def stage(gi, s, staged):
                nc.scalar.copy(idx[:, s, :], src_i[:, at(gi * G, G)]).then_inc(staged, 1)

            with act.If(general < 1):
                for k in range(SL):
                    stage(k, k, s_idx)
            with act.If(general > 0):
                with act.Fori(0, NC) as c:
                    nc.scalar.copy(stg.rearrange("p (b f) -> p b f", b=CB),
                                   hw[:, bass.ds(c * CB, CB), 0:D]).then_inc(s_gst, 1)
                    act.wait_ge(s_gt, c + 1)
                    nc.scalar.copy(hwT[:, bass.ds(c * CW, CW)], bank(0, CW)).then_inc(s_ghw, 1)
            act.wait_ge(s_slog, 1)
            nc.scalar.activation(pself[:], zself[:], ACT.Exp).then_inc(s_sp, 1)

            def windows(gi):
                for k in range(2):
                    n0 = act.value_load(first[0:1, at(gi * G + k * S0, 1)], min_val=0, max_val=N)
                    last = nc.scalar.copy(awin[:, k, :, :],
                                          winT[0:M2, bass.ds(n0, W0)].unsqueeze(1).to_broadcast([M2, 4, W0]))
                last.then_inc(s_awin, 1)

            def transposed(gi, ready, done):
                act.wait_ge(ready, gi + 1)
                nc.scalar.copy(ohT[:].rearrange("p s e -> p (s e)"), bank(0, 2 * P)).then_inc(done, 1)

            def attention(gi, s, nth):
                act.wait_ge(s_log, gi + 1)
                nc.scalar.activation(pt[:, s % 2], zt[:], ACT.Exp).then_inc(s_p, 1)
                if exists(gi + 2):
                    act.wait_ge(s_winp, gi + 2)
                    windows(gi + 2)
                if exists(gi + 1):
                    transposed(gi + 1, s_ohp, s_ohT)
                act.wait_ge(s_msg, gi + 1)
                if exists(gi + SL):
                    stage(gi + SL, s, s_idx)

            act.sem_inc(s_hl, 1)

            def root_b(n):
                root(n + NC + 1, slice(0, 1))

            def normalise_b(n):
                act.wait_ge(s_nmr, n + 3)
                act.wait_ge(s_hfree, n + 1)
                nc.scalar.activation(h1_b, xs[:, at(n * P, P)], ACT.Relu, bias=nmr[:, 0:1],
                                     scale=rinv[:, 0:1]).then_inc(s_hc, 1)

            def copies_b(n):
                blk = at(n * P, P)
                act.wait_ge(s_h1p, n + 1)
                nc.scalar.copy(h1T_b, bank(5, P))
                nc.scalar.copy(h1T[:, blk], bank(5, P)).then_inc(s_h1T, 1)
                act.wait_ge(s_hlp, n + 1)
                nc.scalar.copy(hl[:, blk], bank(6, D)).then_inc(s_hl, 1)

            def block_part(k, n):
                if k == 3:
                    root_b(n)
                    normalise_b(n)
                if k == 4:
                    copies_b(n)

            with act.If(general < 1):
                act.wait_ge(s_prep, 1)
                windows(0)
                transposed(0, s_ohp, s_ohT)
                act.wait_ge(s_winp, 1)
                windows(1)
                groups(act, attention, block_part)
            with act.If(general > 0):
                with act.Fori(0, T) as t:
                    act.wait_ge(s_gz, t + 1)
                    nc.scalar.activation(gp, gz, ACT.Exp).then_inc(s_gp, 1)
                with act.Fori(0, IN_LOOP) as n:
                    root_b(n)
                    normalise_b(n)
                    copies_b(n)
            load_root().then_inc(s_win, 1)
            with act.If(general < 1):
                for k in range(SL):
                    stage(k, k, s_idx1)
            for n in LATE:
                root_b(n)
                act.wait_ge(s_h1p, n)
                normalise_b(n)
            for n in LATE:
                copies_b(n)

            def relational(gi, s, nth):
                if exists(gi + 1):
                    transposed(gi + 1, s_oep, s_oeT)
                if exists(gi + SL):
                    act.wait_ge(s_agg1, gi + 1)
                    stage(gi + SL, s, s_idx1)

            with act.If(general < 1):
                transposed(0, s_oep, s_oeT)
                groups(act, relational)
        @block.vector
        def _(dve):
            def statistics(nth, n, blocks, col):
                if not isinstance(nth, int) or nth:
                    dve.wait_ge(s_var, nth)
                    dve.nop(nofuse=True)
                for k in range(blocks):
                    last = nc.vector.bn_stats(out=stats[:, k, :], in_=xs[:, at((n + k) * D, D)])
                last.then_inc(s_bn, 1)
                dve.wait_ge(s_bn, nth + 1)
                dve.nop(nofuse=True)
                for k in range(blocks):
                    last = nc.vector.bn_aggr(out=mv[:, col + k, :], in_=stats[:, k, :])
                last.then_inc(s_var, 1)

            def scales(nth, blk):
                dve.wait_ge(s_sqrt, nth + 1)
                nc.vector.reciprocal(rinv[:, blk], rstd[:, blk]).then_inc(s_inv, 1)
                dve.wait_ge(s_inv, nth + 1)
                nc.vector.scalar_tensor_tensor(out=nmr[:, blk], in0=mv[:, blk, 0], scalar=-1.0, in1=rinv[:, blk],
                                               op0=ALU.mult, op1=ALU.mult).then_inc(s_nmr, 1)

            nc.vector.memset(eps_t[:], EPS).then_inc(s_vset, 1)
            nc.vector.memset(w_sc[:], 0.0).then_inc(s_vset, 1)
            nc.vector.memset(mark[:, 1:2], 0.0).then_inc(s_scc, 1)
            nc.vector.memset(bad[:], 0.0).then_inc(s_vset, 1)
            nc.vector.memset(high[:], 0.0).then_inc(s_vset, 1)
            nc.vector.memset(low[:], 0.0).then_inc(s_vset, 1)
            nc.vector.memset(winT[0:M2], 0.0).then_inc(s_vset, 1)
            dve.wait_ge(s_x, 16)
            statistics(0, 0, CB, 0)
            scales(0, slice(0, CB))
            dve.wait_ge(s_gset, 9)
            dve.wait_ge(s_att, 16 * 3)
            for k in range(2):
                nc.vector.tensor_tensor(out=att_m[:, k * H:k * H + H], in0=head_of[:],
                                        in1=att_c[:, k:k + 1].to_broadcast([P, H]), op=ALU.mult).then_inc(s_vset, 1)
            nc.vector.tensor_copy(wcat[:, 0:D], w_sb[:]).then_inc(s_vset, 1)
            dve.wait_ge(s_pset, 1)
            nc.vector.tensor_copy(wT[:], bank(0, P)).then_inc(s_vset, 1)
            dve.wait_ge(s_pset, 2)
            nc.vector.tensor_copy(wcat[:, D:HW], bank(1, 2 * H)).then_inc(s_vset, 1)
            for k in (0, 32):
                nc.vector.tensor_copy(w_sc[:, k:k + H], bank(1, H, H)).then_inc(s_vset, 1)
                nc.vector.tensor_copy(w_sc[:, 64 + k:64 + k + H], bank(1, H)).then_inc(s_vset, 1)

            dve.wait_ge(s_xr, 16)
            for c in range(1, NC):
                statistics(c, c * CB, CB, c * CB)
            scales(1, slice(CB, NB))
            dve.wait_ge(s_edges, 16 * EDGE_DMAS)
            for place, shared in ((loc0, S0), (loc1, S1)):
                nc.vector.tensor_tensor(
                    out=place.rearrange("p (k j) -> p k j", j=shared),
                    in0=dst_i.rearrange("p (k j) -> p k j", j=shared),
                    in1=basei.rearrange("p (k j) -> p k j", j=shared)[:, :, 0:1].to_broadcast([P, TT // shared, shared]),
                    op=ALU.subtract).then_inc(s_loc, 1)
            dve.wait_ge(s_loc, 2)
            for part, (rows, lo, hi) in enumerate(((P, 0, E // TILE), (E % TILE, E // TILE, E // TILE + 1))):
                for extreme, op in ((high, ALU.max), (low, ALU.min)):
                    nc.vector.tensor_reduce(out=extreme[0:rows, part, :], in_=loc[0:rows, :, lo:hi], axis=AX.X,
                                            op=op).then_inc(s_vset, 1)
            dve.wait_ge(s_gset, 12)
            nc.vector.tensor_tensor(out=ahead, in0=first[0:1, READY:READY + IN_LOOP * SL * G], in1=behind,
                                    op=ALU.subtract).then_inc(s_loc, 1)
            dve.wait_ge(s_loc, 3)
            nc.vector.tensor_reduce(out=least[:], in_=ahead, axis=AX.X, op=ALU.min).then_inc(s_vset, 1)

            def prepare(c, s):
                dve.wait_ge(s_sc, c + 1)
                scores = bank(5, CW)
                chunk = at(c * CW, CW)
                nc.vector.tensor_copy(dscT[0:M2, chunk], scores[0:M2])
                nc.vector.tensor_copy(sscT[0:M2, chunk], scores[64:64 + M2]).then_inc(s_scc, 1)
                dve.wait_ge(s_scc, c + 2)
                dve.nop(nofuse=True)
                nc.vector.tensor_reduce(out=smc[:, 0, at(c, 1)], in_=sscT[0:M2, chunk], axis=AX.X,
                                        op=ALU.max).then_inc(s_smc, 1)
                nc.vector.tensor_reduce(out=smc[:, 1, at(c, 1)], in_=sscT[0:M2, chunk], axis=AX.X,
                                        op=ALU.min).then_inc(s_smc, 1)

            pairs(dve, prepare)

            dve.wait_ge(s_smc, 2 * NC)
            nc.vector.tensor_reduce(out=smax[:], in_=smc[:, 0, :], axis=AX.X, op=ALU.max).then_inc(s_vset, 1)
            nc.vector.tensor_reduce(out=smin[:], in_=smc[:, 1, :], axis=AX.X, op=ALU.min).then_inc(s_vset, 1)
            dve.wait_ge(s_vset, VS + 7)
            nc.vector.tensor_scalar(out=bad[0:1, 9:10], in0=least[:], scalar1=0.0, scalar2=None,
                                    op0=ALU.is_lt).then_inc(s_vset, 1)
            for k, width in enumerate((W0, W1)):
                nc.vector.tensor_scalar(out=bad[:, 2 * k:2 * k + 2], in0=high[:, :, k], scalar1=width - 1.0,
                                        scalar2=None, op0=ALU.is_gt).then_inc(s_vset, 1)
            nc.vector.tensor_scalar(out=bad[:, 4:8], in0=low[:].rearrange("p a k -> p (a k)"), scalar1=0.0, scalar2=None,
                                    op0=ALU.is_lt).then_inc(s_vset, 1)
            nc.vector.tensor_scalar(out=bad[0:H, 8:9], in0=smax[0:H], scalar1=smin[0:H], scalar2=SPREAD,
                                    op0=ALU.subtract, op1=ALU.is_gt).then_inc(s_vset, 1)
            dve.wait_ge(s_pset, 3)
            nc.vector.tensor_reduce(out=flag_f[:], in_=bank(7, 10)[0:1], axis=AX.X, op=ALU.add).then_inc(s_vset, 1)
            dve.wait_ge(s_vset, VS + 13)
            nc.vector.tensor_scalar(out=flag[:], in0=flag_f[:], scalar1=0.0, scalar2=None,
                                    op0=ALU.is_gt).then_inc(s_flag, 1)
            dve.wait_ge(s_flag, 1)
            general = dve.value_load(flag[0:1, 0:1], min_val=0, max_val=1)

            dve.wait_ge(s_gset, 15)
            with dve.If(general < 1):
                nc.vector.tensor_scalar(out=maxT[0:M2, :], in0=dscT[0:M2, :], scalar1=smax[:], scalar2=None,
                                        op0=ALU.add).then_inc(s_vset, 1)
            with dve.If(general > 0):
                nc.vector.tensor_copy(maxT[0:M2, :], sscT[0:M2, :]).then_inc(s_gv, 1)
                dve.wait_ge(s_gv, 1)
                dve.sem_clear(s_gv)
                with dve.Fori(0, T) as t:
                    with dve.Fori(0, TILE) as e:
                        u = dve.value_load(src_t[bass.ds(e, 1), bass.ds(t, 1)], min_val=0, max_val=N - 1)
                        v = dve.value_load(dst_t[bass.ds(e, 1), bass.ds(t, 1)], min_val=0, max_val=N)
                        nc.vector.tensor_tensor(out=maxT[0:M2, bass.ds(v, 1)], in0=maxT[0:M2, bass.ds(v, 1)],
                                                in1=sscT[0:M2, bass.ds(u, 1)], op=ALU.max).then_inc(s_gv, 1)
                        dve.wait_ge(s_gv, e + 1)
                        dve.nop(nofuse=True)
                    dve.sem_clear(s_gv)
                nc.vector.tensor_tensor(out=maxT[0:M2, :], in0=maxT[0:M2, :], in1=dscT[0:M2, :],
                                        op=ALU.add).then_inc(s_vset, 1)
            dve.wait_ge(s_vset, VS + 14)
            nc.vector.tensor_copy(winT[0:H, :], dscT[0:H, :])
            nc.vector.scalar_tensor_tensor(out=winT[32:M2, :], in0=maxT[32:M2, :], scalar=SLOPE, in1=maxT[32:M2, :],
                                           op0=ALU.mult, op1=ALU.max).then_inc(s_prep, 1)

            nc.vector.tensor_copy(iota[:], iota_i[:]).then_inc(s_v2, 1)
            dve.wait_ge(s_const, 16 * CONST_DMAS)
            nc.vector.tensor_tensor(out=comp_bd[:], in0=quad[:].unsqueeze(2).to_broadcast([P, 4, B]),
                                    in1=comp4[:].unsqueeze(1).to_broadcast([P, 4, B]), op=ALU.mult).then_inc(s_v2, 1)

            dve.wait_ge(s_prjc, NC)
            dve.wait_ge(s_self, 1)
            nc.vector.tensor_tensor(out=zself[:], in0=hw[:, :, D:ROW0], in1=hw[:, :, ROW0:HW],
                                    op=ALU.add).then_inc(s_sv, 1)
            dve.wait_ge(s_sv, 1)
            nc.vector.scalar_tensor_tensor(out=lself[:], in0=zself[:], scalar=SLOPE, in1=zself[:], op0=ALU.mult,
                                           op1=ALU.max).then_inc(s_sv, 1)
            dve.wait_ge(s_sv, 2)
            nc.vector.tensor_tensor(out=zself[:], in0=lself[:], in1=bank(7, NB * H).rearrange("p (b h) -> p b h", b=NB),
                                    op=ALU.subtract).then_inc(s_slog, 1)
            with dve.If(general > 0):
                dve.wait_ge(s_ghw, NC)
            dve.wait_ge(s_tab0, 16 * NC)
            dve.wait_ge(s_sp, 1)
            nc.vector.tensor_tensor(out=hw[:, :, 0:D].rearrange("p b (h c) -> p b h c", h=H),
                                    in0=hw[:, :, 0:D].rearrange("p b (h c) -> p b h c", h=H),
                                    in1=pself[:].unsqueeze(3).to_broadcast([P, NB, H, C]),
                                    op=ALU.mult).then_inc(s_sv, 1)
            xs3 = xs[:, :].rearrange("p (b f) -> p b f", b=NB)
            nc.vector.tensor_tensor(out=xs3, in0=xs3, in1=bias0_b[:].unsqueeze(1).to_broadcast([P, NB, D]),
                                    op=ALU.add).then_inc(s_sv, 1)

            def one_hot0(gi, s):
                nc.vector.tensor_tensor(
                    out=oh[:, s], in0=loc0[:, at(gi * G, G)].unsqueeze(2).to_broadcast([P, G, W0]),
                    in1=iota[:].unsqueeze(1).to_broadcast([P, G, W0]), op=ALU.is_equal).then_inc(s_oh, 1)

            def spread0(gi, s):
                dve.wait_ge(s_winp, gi + 1)
                nc.vector.tensor_tensor(
                    out=bdw[:], in0=bank(1, 4 * H, 64 * s).rearrange("p (k h) -> p k h", k=2).unsqueeze(2)
                    .to_broadcast([P, 2, 4, 2 * H]),
                    in1=quad[:].unsqueeze(1).unsqueeze(3).to_broadcast([P, 2, 4, 2 * H]),
                    op=ALU.mult).then_inc(s_bdw, 1)

            def add0(gi, s):
                n0 = [dve.value_load(first[0:1, at(gi * G + k * S0, 1)], min_val=0, max_val=N) for k in range(2)]
                dve.wait_ge(s_agg, gi + 1)
                for k in range(2):
                    dve.wait_ge(s_a0, gi * 4 + 2 * k + 1)
                    for table, part in ((aggT[:, bass.ds(n0[k], W0)], bank(3 + s, W0, k * W0)),
                                        (denT[0:H, bass.ds(n0[k], W0)], bank(3 + s, W0, (2 + k) * W0)[0:H])):
                        nc.vector.tensor_tensor(out=table, in0=table, in1=part, op=ALU.add).then_inc(s_a0, 1)

            def attention(gi, s, nth):
                if exists(gi + 1):
                    one_hot0(gi + 1, (s + 1) % SL)
                dve.wait_ge(s_ade, gi + 1)
                if exists(gi + 1):
                    spread0(gi + 1, 1 - s % 2)
                dst = ade(s % 2).rearrange("p (t h) -> p t h", t=G)
                dve.wait_ge(got0[s], gathered(gi, nth))
                nc.vector.tensor_tensor(out=zt[:], in0=g0[:, s, :, D:ROW0], in1=dst[:, :, 0:H],
                                        op=ALU.add).then_inc(s_v0, 1)
                dve.wait_ge(s_v0, gi * 3 + 1)
                nc.vector.scalar_tensor_tensor(out=lt[:], in0=zt[:], scalar=SLOPE, in1=zt[:], op0=ALU.mult,
                                               op1=ALU.max).then_inc(s_v0, 1)
                dve.wait_ge(s_v0, gi * 3 + 2)
                nc.vector.tensor_tensor(out=lt[:], in0=lt[:], in1=dst[:, :, H:2 * H],
                                        op=ALU.subtract).then_inc(s_v0, 1)
                dve.wait_ge(s_v0, gi * 3 + 3)
                nc.vector.tensor_scalar(out=zt[:], in0=lt[:], scalar1=0.0, scalar2=None,
                                        op0=ALU.min).then_inc(s_log, 1)
                dve.wait_ge(s_p, gi + 1)
                nc.vector.tensor_tensor(
                    out=msg[:, s % 2].rearrange("p t (h c) -> p t h c", h=H),
                    in0=g0[:, s, :, 0:D].rearrange("p t (h c) -> p t h c", h=H),
                    in1=pt[:, s % 2].unsqueeze(3).to_broadcast([P, G, H, C]), op=ALU.mult).then_inc(s_msg, 1)
                if not is_first(gi):
                    add0(gi - 1, 1 - s % 2)

            dve.wait_ge(s_v2, 2)
            dve.wait_ge(s_sv, 4)

            def stage_b(n):
                nc.vector.tensor_copy(num_b, aggT[:, at(n * P, P)])
                nc.vector.tensor_copy(den_b[0:H], denT[0:H, at(n * P, P)]).then_inc(s_mst, 1)

            def output_b(n):
                xv = xs[:, at(n * P, P)]
                dve.wait_ge(s_mtp, n + 1)
                nc.vector.tensor_tensor(out=den_s[:], in0=pself[:, at(n, 1), :].rearrange("p o h -> p (o h)"),
                                        in1=bank(6, H), op=ALU.add).then_inc(s_vm, 1)
                nc.vector.tensor_tensor(out=row_b, in0=big[:, at(n * HW + 6 * NP, D)], in1=bank(5, D),
                                        op=ALU.add).then_inc(s_vm, 1)
                dve.wait_ge(s_vm, n * 5 + 1)
                nc.vector.reciprocal(rden[:], den_s[:]).then_inc(s_vm, 1)
                dve.wait_ge(s_vm, n * 5 + 3)
                row4 = row_b.rearrange("p (h c) -> p h c", h=H)
                nc.vector.tensor_tensor(out=row4, in0=row4, in1=rden[:].unsqueeze(2).to_broadcast([P, H, C]),
                                        op=ALU.mult).then_inc(s_vm, 1)
                dve.wait_ge(s_vm, n * 5 + 4)
                nc.vector.tensor_tensor(out=xv, in0=xv, in1=row_b, op=ALU.add).then_inc(s_vm, 1)
                dve.wait_ge(s_vm, n * 5 + 5)
                dve.nop(nofuse=True)
                statistics(n + NC, n, 1, 0)

            def scales_b(n):
                dve.wait_ge(s_hc, n + NC)
                scales(n + 2, slice(0, 1))

            def block_part(k, n):
                if k == 2:
                    dve.wait_ge(s_a0, (n + LAG) * (4 * SL) + 9)
                    stage_b(n)
                if k == 3:
                    output_b(n)
                    scales_b(n)

            with dve.If(general < 1):
                nc.vector.memset(mark[:, 5:6], 0.0).then_inc(s_a0, 1)
                one_hot0(0, 0)
                spread0(0, 0)
                groups(dve, attention, block_part)
                add0(NG - 1, 0)
                dve.wait_ge(s_a0, 4 * NG + 1)
            with dve.If(general > 0):
                dve.wait_ge(s_prep, 1)
                nc.vector.scalar_tensor_tensor(out=maxT[0:M2, :], in0=maxT[0:M2, :], scalar=SLOPE,
                                               in1=maxT[0:M2, :], op0=ALU.mult, op1=ALU.max).then_inc(s_gv, 1)
                dve.wait_ge(s_gv, 1)
                dve.sem_clear(s_gv)
                with dve.Fori(0, T) as t:
                    with dve.Fori(0, TILE) as e:
                        u = dve.value_load(src_t[bass.ds(e, 1), bass.ds(t, 1)], min_val=0, max_val=N - 1)
                        v = dve.value_load(dst_t[bass.ds(e, 1), bass.ds(t, 1)], min_val=0, max_val=N)
                        nc.vector.tensor_tensor(out=gz[:, bass.ds(e, 1)], in0=sscT[0:H, bass.ds(u, 1)],
                                                in1=dscT[0:H, bass.ds(v, 1)], op=ALU.add)
                        nc.vector.tensor_copy(gm[:, bass.ds(e, 1)], maxT[0:H, bass.ds(v, 1)]).then_inc(s_gv, 1)
                    dve.wait_ge(s_gv, TILE)
                    nc.vector.scalar_tensor_tensor(out=gz, in0=gz, scalar=SLOPE, in1=gz, op0=ALU.mult,
                                                   op1=ALU.max).then_inc(s_gv, 1)
                    dve.wait_ge(s_gv, TILE + 1)
                    nc.vector.tensor_tensor(out=gz, in0=gz, in1=gm, op=ALU.subtract).then_inc(s_gz, 1)
                    dve.wait_ge(s_gb, t + 1)
                    dve.nop(nofuse=True)
                    dve.sem_clear(s_gv)
                    with dve.Fori(0, TILE) as e:
                        u = dve.value_load(src_t[bass.ds(e, 1), bass.ds(t, 1)], min_val=0, max_val=N - 1)
                        v = dve.value_load(dst_t[bass.ds(e, 1), bass.ds(t, 1)], min_val=0, max_val=N)
                        nc.vector.tensor_tensor(out=denT[0:H, bass.ds(v, 1)], in0=denT[0:H, bass.ds(v, 1)],
                                                in1=gp[:, bass.ds(e, 1)], op=ALU.add)
                        nc.vector.scalar_tensor_tensor(
                            out=aggT[:, bass.ds(v, 1)], in0=hwT[:, bass.ds(u, 1)], scalar=ps[:, bass.ds(e, 1)],
                            in1=aggT[:, bass.ds(v, 1)], op0=ALU.mult, op1=ALU.add).then_inc(s_gv, 1)
                        dve.wait_ge(s_gv, e + 1)
                        dve.nop(nofuse=True)
                    dve.sem_clear(s_gv)
                with dve.Fori(0, IN_LOOP) as n:
                    stage_b(n)
                    output_b(n)
                    scales_b(n)
            nc.vector.memset(mark[:, 0:1], 0.0).then_inc(s_l0, 1)


            stage_b(LATE[0])
            output_b(LATE[0])
            stage_b(LATE[1])
            scales_b(LATE[0])
            output_b(LATE[1])
            scales_b(LATE[1])

            def select1(gi, s):
                nc.vector.tensor_tensor(
                    out=oh[:, 0], in0=typ_f[:, at(gi * G, G)].unsqueeze(2).to_broadcast([P, G, R]),
                    in1=iota[:].unsqueeze(1).to_broadcast([P, G, R]), op=ALU.is_equal).then_inc(s_oe, 1)
                if not is_first(gi):
                    dve.wait_ge(s_sel, gi)
                nc.vector.tensor_tensor(
                    out=oh1[:], in0=loc1[:, at(gi * G, G)].unsqueeze(2).to_broadcast([P, G, W1]),
                    in1=iota[:, 0:W1].unsqueeze(1).to_broadcast([P, G, W1]), op=ALU.is_equal).then_inc(s_v1, 1)
                dve.wait_ge(s_cop, gi + 1)
                nc.vector.tensor_tensor(
                    out=coef[:], in0=bank(1, G * B).rearrange("p (t b) -> p t b", t=G),
                    in1=wgt[:, at(gi * G, G)].unsqueeze(2).to_broadcast([P, G, B]), op=ALU.mult).then_inc(s_v1, 1)
                dve.wait_ge(s_v1, gi * 2 + 2)
                nc.vector.tensor_tensor(
                    out=sel1[:, s], in0=oh1[:].unsqueeze(2).to_broadcast([P, G, B, W1]),
                    in1=coef[:].unsqueeze(3).to_broadcast([P, G, B, W1]), op=ALU.mult).then_inc(s_sel, 1)

            def relational(gi, s, nth):
                if exists(gi + 1):
                    select1(gi + 1, 1 - s % 2)
                n0 = [dve.value_load(first[0:1, at(gi * G + k * S1, 1)], min_val=0, max_val=N)
                      for k in range(G // S1)]
                dve.wait_ge(s_agg1, gi + 1)
                for k in range(G // S1):
                    if k or not is_first(gi):
                        dve.wait_ge(s_a1, gi * 4 + k)
                    table = agg1[:, :, bass.ds(n0[k], W1)]
                    nc.vector.tensor_tensor(
                        out=table, in0=table,
                        in1=bank(2 + s % 2, B * W1, k * B * W1).rearrange("p (b w) -> p b w", b=B),
                        op=ALU.add).then_inc(s_a1, 1)

            nc.vector.memset(mark[:, 3:4], 0.0).then_inc(s_fv, 1)

            def stage_block(n, into=aggc):
                nc.vector.tensor_copy(into, agg1[:, :, at(n * P, P)]).then_inc(s_fst, 1)

            def finish(n, bank_no=4):
                blk = at(n * P, P)
                dve.wait_ge(s_fp, n + 2)
                nc.vector.tensor_tensor(out=pre, in0=hl[:, blk], in1=bank(bank_no, D), op=ALU.add).then_inc(s_fv, 1)
                dve.wait_ge(s_fv, n + 2)
                dve.wait_ge(s_ofree, n + 1)
                nc.vector.scalar_tensor_tensor(out=outc, in0=pre, scalar=0.0, in1=xs[:, blk], op0=ALU.max,
                                               op1=ALU.add).then_inc(s_fo, 1)

            def block_part(k, n):
                if k == 1:
                    dve.wait_ge(s_a1, (n + LAG) * (4 * SL) + 8)
                    dve.wait_ge(s_fp, n + 1)
                    stage_block(n)
                if k == 3:
                    finish(n)

            nc.vector.memset(big[:, 0:2 * NP], 0.0).then_inc(s_zero, 1)
            with dve.If(general < 1):
                select1(0, 0)
            nc.vector.memset(big[:, 4 * NP:B * NP], 0.0).then_inc(s_zero, 1)
            dve.wait_ge(s_hl, NB + 1)
            dve.wait_ge(s_zero, 2)
            dve.wait_ge(s_zrest, 1)
            with dve.If(general < 1):
                groups(dve, relational, block_part)
                dve.wait_ge(s_a1, 4 * NG)
            with dve.If(general > 0):
                with dve.Fori(0, T) as t:
                    nc.vector.tensor_tensor(out=oh[:, 0, 0, :], in0=typ_f[:, bass.ds(t, 1)].to_broadcast([P, R]),
                                            in1=iota[:], op=ALU.is_equal).then_inc(s_oe, 1)
                    dve.wait_ge(s_oep, t + 1)
                    nc.vector.tensor_copy(ohT[0:R, 0, :], bank(0, P)[0:R]).then_inc(s_oeT, 1)
                    dve.wait_ge(s_cop, t + 1)
                    nc.vector.tensor_tensor(out=coef[:, 0, :], in0=bank(1, B),
                                            in1=wgt[:, bass.ds(t, 1)].to_broadcast([P, B]),
                                            op=ALU.mult).then_inc(s_gc, 1)
                    dve.wait_ge(s_gr, t * 16 + 16)
                    dve.nop(nofuse=True)
                    with dve.Fori(0, TILE) as e:
                        u = dve.value_load(src_t[bass.ds(e, 1), bass.ds(t, 1)], min_val=0, max_val=N - 1)
                        v = dve.value_load(dst_t[bass.ds(e, 1), bass.ds(t, 1)], min_val=0, max_val=N)
                        nc.vector.scalar_tensor_tensor(
                            out=agg1[:, :, bass.ds(v, 1)].rearrange("p b o -> p (b o)"), in0=gcb[:, bass.ds(e * B, B)],
                            scalar=h1T[:, bass.ds(u, 1)],
                            in1=agg1[:, :, bass.ds(v, 1)].rearrange("p b o -> p (b o)"), op0=ALU.mult,
                            op1=ALU.add).then_inc(s_gv, 1)
                        dve.wait_ge(s_gv, e + 1)
                        dve.nop(nofuse=True)
                    dve.sem_clear(s_gv)
                with dve.Fori(0, IN_LOOP) as n:
                    dve.wait_ge(s_fp, n + 1)
                    stage_block(n)
                    finish(n)
            stage_block(LATE[0])
            stage_block(LATE[1], aggc_late)
            finish(LATE[0])
            dve.wait_ge(s_fo, LATE[1])
            finish(LATE[1], 5)

        @block.tensor
        def _(pe):
            mm, tr = nc.tensor.matmul, nc.tensor.transpose

            def cols(at, n, rows=P):
                return ps[0:rows, at:at + n]

            def blocks(src, col):
                for k in range(CB):
                    last = tr(cols(col + k * P, P), src[:, k * P:k * P + P], ident[:])
                return last

            pe.wait_ge(s_att, 16 * 3)
            pe.wait_ge(s_gset, 3)
            tr(cols(0, P), w_sb[:], ident[:]).then_inc(s_pset, 1)
            pe.wait_ge(s_vset, 10)
            mm(cols(512, 2 * H), wT[:], att_m[:], start=True, stop=True).then_inc(s_pset, 1)
            pe.wait_ge(s_vset, VS)
            def prepare(c, s):
                pe.wait_ge(s_hc, c + 1)
                blocks(hc[:, s], 0).then_inc(s_hcp, 1)
                pe.wait_ge(s_hcT, c + 1)
                for k in range(CB):
                    last = mm(cols(1024 + k * 256, HW), hcT[:, k * P:k * P + P], wcat[:], start=True, stop=True)
                last.then_inc(s_prj, 1)
                pe.wait_ge(s_scc, c + 1)
                for lo, hi in ((0, 512), (512, CW)):
                    last = mm(cols(5 * 512 + lo, hi - lo, 64 + M2), w_sc[:], hcT[:, lo:hi], start=True, stop=True)
                last.then_inc(s_sc, 1)

            pairs(pe, prepare)
            pe.wait_ge(s_vset, VS + 12)
            mm(cols(7 * 512, 10, 1), ones[:, 0:1], bad[:], start=True, stop=True).then_inc(s_pset, 1)
            pe.wait_ge(s_flag, 1)
            general = pe.value_load(flag[0:1, 0:1], min_val=0, max_val=1)

            with pe.If(general > 0):
                with pe.Fori(0, NC) as c:
                    pe.wait_ge(s_gst, c + 1)
                    blocks(stg, 0).then_inc(s_gt, 1)
            pe.wait_ge(s_prep, 1)
            for b in range(NB):
                last = tr(cols(7 * 512 + b * H, H), winT[32:M2, b * P:b * P + P], ident[32:M2, 32:M2])
            last.then_inc(s_self, 1)

            def turn(gi, s, ready, done):
                pe.wait_ge(ready, gi + 1)
                for k in range(2):
                    last = tr(cols(k * P, P), oh[:, s, k * 4:k * 4 + 4, :].rearrange("p t w -> p (t w)"), ident[:])
                last.then_inc(done, 1)

            def window0(gi, s):
                pe.wait_ge(s_awin, gi + 1)
                for k in range(2):
                    last = mm(cols(512 + 64 * s + k * 2 * H, 2 * H), awin[:, k].rearrange("p q w -> p (q w)"), pick[:],
                              start=True, stop=True)
                last.then_inc(s_winp, 1)

            def scores0(gi, s):
                pe.wait_ge(s_ohT, gi + 1)
                pe.wait_ge(s_bdw, gi + 1)
                for k in range(2):
                    last = mm(ade(s)[:, k * 8 * H:k * 8 * H + 8 * H], ohT[:, k, :], bdw[:, k].rearrange("p q h -> p (q h)"),
                              start=True, stop=True)
                last.then_inc(s_ade, 1)

            def attention(gi, s, nth):
                if exists(gi + 1):
                    turn(gi + 1, (s + 1) % SL, s_oh, s_ohp)
                if exists(gi + 2):
                    pe.wait_ge(s_bdw, gi + 2)
                    window0(gi + 2, s % 2)
                if exists(gi + 1):
                    scores0(gi + 1, 1 - s % 2)
                pe.wait_ge(s_msg, gi + 1)
                for k in range(2):
                    for j in range(S0):
                        t = k * S0 + j
                        mm(cols((3 + s % 2) * 512 + k * W0, W0), msg[:, s % 2, t, :], oh[:, s, t, :], start=(j == 0),
                           stop=(j == S0 - 1))
                    for j in range(S0):
                        t = k * S0 + j
                        last = mm(cols((3 + s % 2) * 512 + (2 + k) * W0, W0, H), pt[:, s % 2, t, :], oh[:, s, t, :],
                                  start=(j == 0), stop=(j == S0 - 1))
                last.then_inc(s_agg, 1)

            pe.wait_ge(s_const, 16 * CONST_DMAS)

            def sums_b(n):
                pe.wait_ge(s_mst, n + 1)
                tr(cols(5 * 512, P), num_b, ident[:])
                tr(cols(6 * 512, H), den_b[0:H], ident[0:H, 0:H]).then_inc(s_mtp, 1)

            def features_b(n):
                pe.wait_ge(s_hc, n + NC + 1)
                tr(cols(5 * 512, P), h1_b, ident[:]).then_inc(s_h1p, 1)
                pe.wait_ge(s_h1T, n + 1)
                mm(cols(6 * 512, D), h1T_b, loop_sb[:], start=True, stop=False)
                mm(cols(6 * 512, D), ones[0:1, :], bias1_b[0:1, :], start=False, stop=True).then_inc(s_hlp, 1)

            def block_part(k, n):
                if k == 2:
                    pe.wait_ge(s_hl, n + 1)
                    sums_b(n)
                if k == 4:
                    features_b(n)

            with pe.If(general < 1):
                turn(0, 0, s_oh, s_ohp)
                window0(0, 0)
                scores0(0, 0)
                window0(1, 1)
                groups(pe, attention, block_part)
            with pe.If(general > 0):
                with pe.Fori(0, T) as t:
                    pe.wait_ge(s_gp, t + 1)
                    mm(cols(0, TILE), head_to[:], gp, start=True, stop=True).then_inc(s_gb, 1)
                with pe.Fori(0, IN_LOOP) as n:
                    pe.wait_ge(s_hl, n + 1)
                    sums_b(n)
                    features_b(n)

            pe.wait_ge(s_hl, IN_LOOP + 1)
            for n in LATE:
                sums_b(n)
            pe.wait_ge(s_vm, LATE[1] * 5 + 2)
            for n in LATE:
                features_b(n)
            pe.wait_ge(s_v2, 2)

            def coefs1(gi):
                turn(gi, 0, s_oe, s_oep)
                pe.wait_ge(s_oeT, gi + 1)
                for k in range(2):
                    last = mm(cols(512 + k * 4 * B, 4 * B), ohT[:, k, :], comp_bd[:].rearrange("p q b -> p (q b)"),
                              start=True, stop=True)
                last.then_inc(s_cop, 1)

            def relational(gi, s, nth):
                if exists(gi + 1):
                    coefs1(gi + 1)
                pe.wait_ge(s_sel, gi + 1)
                pe.wait_ge(got1[s], gathered(gi, nth))
                for t in range(G):
                    last = mm(cols((2 + s % 2) * 512 + t // S1 * B * W1, B * W1), g1[:, s, t, :],
                              sel1[:, s % 2, t].rearrange("p b w -> p (b w)"), start=(t % S1 == 0),
                              stop=(t % S1 == S1 - 1))
                last.then_inc(s_agg1, 1)

            pe.sem_inc(s_fp, 1)

            def product(n, sums=aggc, bank_no=4):
                pe.wait_ge(s_fst, n + 1)
                for b in range(B):
                    last = mm(cols(bank_no * 512, D), sums[:, b, :], basis_sb[:, b, :], start=(b == 0),
                              stop=(b == B - 1))
                last.then_inc(s_fp, 1)

            def block_part(k, n):
                if k == 2:
                    pe.wait_ge(s_fv, n + 1)
                    product(n)

            with pe.If(general < 1):
                coefs1(0)
                groups(pe, relational, block_part)
            with pe.If(general > 0):
                with pe.Fori(0, T) as t:
                    pe.wait_ge(s_oe, t + 1)
                    tr(cols(0, P, R), oh[:, 0, 0, :], ident[:]).then_inc(s_oep, 1)
                    pe.wait_ge(s_oeT, t + 1)
                    mm(cols(512, B), ohT[0:R, 0, :], comp4[0:R, :], start=True, stop=True).then_inc(s_cop, 1)
                with pe.Fori(0, IN_LOOP) as n:
                    pe.wait_ge(s_fv, n + 1)
                    product(n)

            pe.wait_ge(s_fv, IN_LOOP + 1)
            product(LATE[0])
            product(LATE[1], aggc_late, 5)


def kernel(x, src, dst, edge_type_32, edge_weight1, L0_gnn_W, L0_gnn_att_src, L0_gnn_att_dst, L0_gnn_bias,
           L1_gnn_weight, L1_gnn_w_comp, L1_gnn_loop_weight, L1_gnn_h_bias):
    import numpy as np
    import concourse.bacc as bacc
    from concourse.bass_utils import run_bass_kernel_spmd

    def tiles(a, pad, n):
        full = np.full(n * TILE, pad, a.dtype)
        full[:E] = a.reshape(-1)
        return np.ascontiguousarray(full.reshape(n, TILE).T)

    xp = np.zeros((NP, D), x.dtype)
    xp[:N] = x
    arrays = {
        "x_pad": xp, "src_t": tiles(src, 0, TT), "dst_t": tiles(dst, N, TT),
        "typ_t": tiles(edge_type_32, 0, TT), "wgt_t": tiles(edge_weight1, 0, TT), "w_att": L0_gnn_W,
        "att_src": L0_gnn_att_src, "att_dst": L0_gnn_att_dst, "bias0": L0_gnn_bias, "basis": L1_gnn_weight,
        "w_comp": L1_gnn_w_comp, "w_loop": L1_gnn_loop_weight, "bias1": L1_gnn_h_bias,
    }
    nc = bacc.Bacc("TRN2", target_bir_lowering=False, num_devices=1)
    arrays = {k: np.ascontiguousarray(v) for k, v in arrays.items()}
    args = [nc.dram_tensor(k, v.shape, mybir.dt.from_np(v.dtype), kind="ExternalInput").ap()
            for k, v in arrays.items()]
    out = nc.dram_tensor("out", (NP, D), mybir.dt.float32, kind="ExternalOutput").ap()
    build(nc, *args, out)
    res = run_bass_kernel_spmd(nc, [arrays], core_ids=[0])
    return res.results[0]["out"][:N]
```
